# Optimizing a Trainium2 kernel written in Bass

```python
import numpy as np
import jax
import jax.numpy as jnp

def _softmax(x, axis=-1):
    return jax.nn.softmax(x, axis=axis)

def _gelu(x):
    return jax.nn.gelu(x, approximate=True)

def _silu(x):
    return jax.nn.silu(x)

def _sigmoid(x):
    return jax.nn.sigmoid(x)

def _layernorm(x, axis=-1, eps=1e-05):
    m = jnp.mean(x, axis=axis, keepdims=True)
    v = jnp.var(x, axis=axis, keepdims=True)
    return (x - m) / jnp.sqrt(v + eps)

def _scatter_add(tgt, idx, src, axis=0):
    return tgt.at[idx].add(src)

def _segment_sum(src, seg, n):
    return jax.ops.segment_sum(src, seg, n)
kernel_name = 'mk_perceiver_d1_seqx_r8_c0bf85'

def setup_inputs(seed: int=0):
    np.random.seed(seed)
    _w = jnp.asarray

    def _rec_inputs():
        import jax
        import jax.numpy as jnp
        _rk = jax.random.key(seed)
        x = 7.22e-05 + 1 * jax.random.normal(jax.random.fold_in(_rk, 1), (32, 64, 128), jnp.float32)
        _lenS = 64 - jax.random.randint(jax.random.fold_in(_rk, 7), (32,), 0, max(1, 64 // 4) + 1, jnp.int32)
        _lenS2 = 1601 - jax.random.randint(jax.random.fold_in(_rk, 8), (32,), 0, max(1, 1601 // 4) + 1, jnp.int32)
        _ctx_1024P = jax.random.normal(jax.random.fold_in(_rk, 11), (32, 16, 128), jnp.float32)
        _ctx_1024c = jax.random.dirichlet(jax.random.fold_in(_rk, 511), 0.3 * jnp.ones((16,), jnp.float32), (32, 1601))
        _ctx_1024t = jnp.einsum('bsk,bkd->bsd', _ctx_1024c, _ctx_1024P)
        _ctx_1024t = _ctx_1024t * jax.lax.rsqrt(jnp.mean(jnp.square(_ctx_1024t)) + 1e-12) * 0.953939
        ctx_1024 = 4.13588e-05 + 0.999923 * (_ctx_1024t + 0.3 * jax.random.normal(jax.random.fold_in(_rk, 611), (32, 1601, 128), jnp.float32))
        return (x, ctx_1024)
    x, ctx_1024 = _rec_inputs()

    def _L0_xattn_setup():
        import jax, jax.numpy as jnp
        import numpy as np
        B, L, D_MODEL, H, DK, DV = (4, 256, 128, 16, 64, 64)
        key = jax.random.key(seed)
        ks = jax.random.split(key, 11)
        s = 1.0 / np.sqrt(D_MODEL)
        return {'queries': jax.random.normal(ks[0], (B, L, D_MODEL), jnp.float32), 'keys': jax.random.normal(ks[1], (B, L, D_MODEL), jnp.float32), 'values': jax.random.normal(ks[2], (B, L, D_MODEL), jnp.float32), 'Wq': jax.random.normal(ks[3], (D_MODEL, H * DK), jnp.float32) * s, 'bq': jnp.zeros((H * DK,), jnp.float32), 'Wk': jax.random.normal(ks[4], (D_MODEL, H * DK), jnp.float32) * s, 'bk': jnp.zeros((H * DK,), jnp.float32), 'Wv': jax.random.normal(ks[5], (D_MODEL, H * DV), jnp.float32) * s, 'bv': jnp.zeros((H * DV,), jnp.float32), 'Wo': jax.random.normal(ks[6], (H * DV, D_MODEL), jnp.float32) * s, 'bo': jnp.zeros((D_MODEL,), jnp.float32)}
    _L0_xattn_all = _L0_xattn_setup()
    _L0_xattn_in = {k: v for k, v in _L0_xattn_all.items() if k in ('Wq', 'bq', 'Wk', 'bk', 'Wv', 'bv', 'Wo', 'bo')}
    del _L0_xattn_all

    def _L0_attn_setup():
        import jax, jax.numpy as jnp
        import numpy as np
        N_EMBD = 128
        N_HEAD = 16
        N_LAYER = 24
        LAYER_ID = 12
        B, T = (4, 512)
        Q = 64
        EPS = 1e-05 * 64

        def _static_params():
            C, H = (N_EMBD, N_HEAD)
            r01 = LAYER_ID / (N_LAYER - 1)
            r1a0 = 1.0 - LAYER_ID / N_LAYER
            ddd = np.arange(C, dtype=np.float64) / C
            maa_k = (1.0 - ddd ** r1a0).astype(np.float32).reshape(1, 1, C)
            maa_v = (1.0 - (ddd ** r1a0 + 0.3 * r01)).astype(np.float32).reshape(1, 1, C)
            maa_r = (1.0 - ddd ** (0.5 * r1a0)).astype(np.float32).reshape(1, 1, C)
            maa_g = maa_r.copy()
            h = np.arange(H, dtype=np.float64)
            decay = (-6.0 + 5.0 * (h / (H - 1)) ** (0.7 + 1.3 * r01)).astype(np.float32).reshape(H, 1)
            faaaa = (r01 * (1.0 - h / (H - 1))).astype(np.float32).reshape(H, 1)
            return (maa_k, maa_v, maa_r, maa_g, decay, faaaa)

        def _rwkv_forward(x, time_maa_k, time_maa_v, time_maa_r, time_maa_g, time_decay, time_faaaa, Wr, Wk, Wv, Wg, Wo, ln_w, ln_b):
            Bv, Tv, C = x.shape
            H = N_HEAD
            N = C // H
            nC = Tv // Q
            xx = jnp.pad(x, ((0, 0), (1, 0), (0, 0)))[:, :Tv] - x
            xk = x + xx * time_maa_k
            xv = x + xx * time_maa_v
            xr = x + xx * time_maa_r
            xg = x + xx * time_maa_g
            r = (xr @ Wr.T).reshape(Bv, Tv, H, N).transpose(0, 2, 1, 3)
            k = (xk @ Wk.T).reshape(Bv, Tv, H, N).transpose(0, 2, 3, 1)
            v = (xv @ Wv.T).reshape(Bv, Tv, H, N).transpose(0, 2, 1, 3)
            g = jax.nn.gelu(xg @ Wg.T, approximate=False)
            w = jnp.exp(-jnp.exp(time_decay))[:, 0]
            u = time_faaaa[:, 0]
            q = jnp.arange(Q)
            ws = (w ** Q).reshape(1, H, 1, 1)
            wk = (w[:, None] ** (Q - 1 - q)).reshape(1, H, 1, Q)
            wb = (w[:, None] ** q).reshape(1, H, Q, 1)
            i_idx = q[:, None]
            j_idx = q[None, :]
            e = jnp.maximum(i_idx - j_idx - 1, 0)
            Wmat = jnp.where(i_idx > j_idx, w[:, None, None] ** e, 0.0)
            Wmat = Wmat + jnp.eye(Q, dtype=x.dtype) * u[:, None, None]
            Wmat = Wmat.reshape(1, H, Q, Q)
            rr = r.reshape(Bv, H, nC, Q, N).transpose(2, 0, 1, 3, 4)
            kk = k.reshape(Bv, H, N, nC, Q).transpose(3, 0, 1, 2, 4)
            vv = v.reshape(Bv, H, nC, Q, N).transpose(2, 0, 1, 3, 4)

            def step(state, inp):
                rc, kc, vc = inp
                att = rc @ kc
                yc = att * Wmat @ vc + rc @ state * wb
                new_state = ws * state + kc * wk @ vc
                return (new_state, yc)
            state0 = jnp.zeros((Bv, H, N, N), dtype=x.dtype)
            _, ys = jax.lax.scan(step, state0, (rr, kk, vv))
            y = ys.transpose(1, 2, 0, 3, 4).reshape(Bv, H, Tv, N)
            y = y.transpose(0, 2, 1, 3)
            mean = y.mean(axis=-1, keepdims=True)
            var = y.var(axis=-1, keepdims=True)
            yn = (y - mean) / jnp.sqrt(var + EPS)
            yn = yn * ln_w.reshape(1, 1, H, N) + ln_b.reshape(1, 1, H, N)
            yn = yn.reshape(Bv, Tv, C)
            out = yn * g @ Wo.T
            return out
        key = jax.random.key(seed)
        ks = jax.random.split(key, 8)
        C = N_EMBD
        maa_k, maa_v, maa_r, maa_g, decay, faaaa = _static_params()
        std = 0.02
        return {'x': jax.random.normal(ks[0], (B, T, C), dtype=jnp.float32), 'time_maa_k': jnp.asarray(maa_k), 'time_maa_v': jnp.asarray(maa_v), 'time_maa_r': jnp.asarray(maa_r), 'time_maa_g': jnp.asarray(maa_g), 'time_decay': jnp.asarray(decay), 'time_faaaa': jnp.asarray(faaaa), 'Wr': jax.random.normal(ks[1], (C, C), dtype=jnp.float32) * std, 'Wk': jax.random.normal(ks[2], (C, C), dtype=jnp.float32) * std, 'Wv': jax.random.normal(ks[3], (C, C), dtype=jnp.float32) * std, 'Wg': jax.random.normal(ks[4], (C, C), dtype=jnp.float32) * std, 'Wo': jax.random.normal(ks[5], (C, C), dtype=jnp.float32) * std, 'ln_w': jnp.ones((C,), dtype=jnp.float32), 'ln_b': jnp.zeros((C,), dtype=jnp.float32)}
    _L0_attn_all = _L0_attn_setup()
    _L0_attn_in = {k: v for k, v in _L0_attn_all.items() if k in ('time_maa_k', 'time_maa_v', 'time_maa_r', 'time_maa_g', 'time_decay', 'time_faaaa', 'Wr', 'Wk', 'Wv', 'Wg', 'Wo', 'ln_w', 'ln_b')}
    del _L0_attn_all

    def _L0_ffn_setup():
        import jax, jax.numpy as jnp
        import numpy as np
        EPS = 1e-06
        LN_EPS = 1e-05

        def _absmean_core(W):
            gamma = jnp.mean(jnp.abs(W)) + EPS
            Ws = W / gamma
            Wq = jnp.sign(Ws) * jnp.minimum(jnp.round(jnp.abs(Ws)), 1.0)
            return (Wq, gamma)

        @jax.custom_vjp
        def absmean(W):
            return _absmean_core(W)[0]

        def _absmean_fwd(W):
            Wq, gamma = _absmean_core(W)
            return (Wq, gamma)

        def _absmean_bwd(gamma, g):
            return (g / gamma,)
        absmean.defvjp(_absmean_fwd, _absmean_bwd)

        def layernorm(x, w, b, eps=LN_EPS):
            mu = jnp.mean(x, axis=-1, keepdims=True)
            var = jnp.mean((x - mu) ** 2, axis=-1, keepdims=True)
            return (x - mu) * jax.lax.rsqrt(var + eps) * w + b
        key = jax.random.key(seed)
        k1, k2, k3 = jax.random.split(key, 3)
        d, h = (128, 512)
        B, T = (8, 256)
        return {'x': jax.random.normal(k1, (B, T, d), jnp.float32), 'W_fc': jax.random.normal(k2, (h, d), jnp.float32), 'ln_w': jnp.ones((h,), jnp.float32), 'ln_b': jnp.zeros((h,), jnp.float32), 'W_proj': jax.random.normal(k3, (d, h), jnp.float32)}
    _L0_ffn_all = _L0_ffn_setup()
    _L0_ffn_in = {k: v for k, v in _L0_ffn_all.items() if k in ('W_fc', 'ln_w', 'ln_b', 'W_proj')}
    del _L0_ffn_all
    return {'x': x, 'ctx_1024': ctx_1024, 'L0_xattn_Wq': _L0_xattn_in['Wq'], 'L0_xattn_bq': _L0_xattn_in['bq'], 'L0_xattn_Wk': _L0_xattn_in['Wk'], 'L0_xattn_bk': _L0_xattn_in['bk'], 'L0_xattn_Wv': _L0_xattn_in['Wv'], 'L0_xattn_bv': _L0_xattn_in['bv'], 'L0_xattn_Wo': _L0_xattn_in['Wo'], 'L0_xattn_bo': _L0_xattn_in['bo'], 'L0_attn_time_maa_k': _L0_attn_in['time_maa_k'], 'L0_attn_time_maa_v': _L0_attn_in['time_maa_v'], 'L0_attn_time_maa_r': _L0_attn_in['time_maa_r'], 'L0_attn_time_maa_g': _L0_attn_in['time_maa_g'], 'L0_attn_time_decay': _L0_attn_in['time_decay'], 'L0_attn_time_faaaa': _L0_attn_in['time_faaaa'], 'L0_attn_Wr': _L0_attn_in['Wr'], 'L0_attn_Wk': _L0_attn_in['Wk'], 'L0_attn_Wv': _L0_attn_in['Wv'], 'L0_attn_Wg': _L0_attn_in['Wg'], 'L0_attn_Wo': _L0_attn_in['Wo'], 'L0_attn_ln_w': _L0_attn_in['ln_w'], 'L0_attn_ln_b': _L0_attn_in['ln_b'], 'L0_ffn_W_fc': _L0_ffn_in['W_fc'], 'L0_ffn_ln_w': _L0_ffn_in['ln_w'], 'L0_ffn_ln_b': _L0_ffn_in['ln_b'], 'L0_ffn_W_proj': _L0_ffn_in['W_proj']}

def reference(x, ctx_1024, L0_xattn_Wq, L0_xattn_bq, L0_xattn_Wk, L0_xattn_bk, L0_xattn_Wv, L0_xattn_bv, L0_xattn_Wo, L0_xattn_bo, L0_attn_time_maa_k, L0_attn_time_maa_v, L0_attn_time_maa_r, L0_attn_time_maa_g, L0_attn_time_decay, L0_attn_time_faaaa, L0_attn_Wr, L0_attn_Wk, L0_attn_Wv, L0_attn_Wg, L0_attn_Wo, L0_attn_ln_w, L0_attn_ln_b, L0_ffn_W_fc, L0_ffn_ln_w, L0_ffn_ln_b, L0_ffn_W_proj):
    import jax
    import jax.numpy as jnp

    def _L0_xattn_ref(queries, keys, values, Wq, bq, Wk, bk, Wv, bv, Wo, bo):
        import jax, jax.numpy as jnp
        import numpy as np
        B, L, D_MODEL, H, DK, DV = (4, 256, 128, 16, 64, 64)
        b, l, _ = queries.shape
        s = keys.shape[1]
        q = (queries @ Wq + bq).reshape(b, l, H, DK)
        k = (keys @ Wk + bk).reshape(b, s, H, DK)
        v = (values @ Wv + bv).reshape(b, s, H, DV)
        scale = 1.0 / np.sqrt(DK)
        scores = jnp.einsum('blhe,bshe->bhls', q, k)
        causal = jnp.triu(jnp.ones((l, s), bool), k=1)
        scores = jnp.where(causal[None, None], -jnp.inf, scores)
        A = jax.nn.softmax(scale * scores, axis=-1)
        out = jnp.einsum('bhls,bshd->blhd', A, v).reshape(b, l, H * DV)
        return out @ Wo + bo

    def _L0_attn_ref(x, time_maa_k, time_maa_v, time_maa_r, time_maa_g, time_decay, time_faaaa, Wr, Wk, Wv, Wg, Wo, ln_w, ln_b):
        import jax, jax.numpy as jnp
        import numpy as np
        N_EMBD = 128
        N_HEAD = 16
        N_LAYER = 24
        LAYER_ID = 12
        B, T = (4, 512)
        Q = 64
        EPS = 1e-05 * 64

        def _static_params():
            C, H = (N_EMBD, N_HEAD)
            r01 = LAYER_ID / (N_LAYER - 1)
            r1a0 = 1.0 - LAYER_ID / N_LAYER
            ddd = np.arange(C, dtype=np.float64) / C
            maa_k = (1.0 - ddd ** r1a0).astype(np.float32).reshape(1, 1, C)
            maa_v = (1.0 - (ddd ** r1a0 + 0.3 * r01)).astype(np.float32).reshape(1, 1, C)
            maa_r = (1.0 - ddd ** (0.5 * r1a0)).astype(np.float32).reshape(1, 1, C)
            maa_g = maa_r.copy()
            h = np.arange(H, dtype=np.float64)
            decay = (-6.0 + 5.0 * (h / (H - 1)) ** (0.7 + 1.3 * r01)).astype(np.float32).reshape(H, 1)
            faaaa = (r01 * (1.0 - h / (H - 1))).astype(np.float32).reshape(H, 1)
            return (maa_k, maa_v, maa_r, maa_g, decay, faaaa)

        def _rwkv_forward(x, time_maa_k, time_maa_v, time_maa_r, time_maa_g, time_decay, time_faaaa, Wr, Wk, Wv, Wg, Wo, ln_w, ln_b):
            Bv, Tv, C = x.shape
            H = N_HEAD
            N = C // H
            nC = Tv // Q
            xx = jnp.pad(x, ((0, 0), (1, 0), (0, 0)))[:, :Tv] - x
            xk = x + xx * time_maa_k
            xv = x + xx * time_maa_v
            xr = x + xx * time_maa_r
            xg = x + xx * time_maa_g
            r = (xr @ Wr.T).reshape(Bv, Tv, H, N).transpose(0, 2, 1, 3)
            k = (xk @ Wk.T).reshape(Bv, Tv, H, N).transpose(0, 2, 3, 1)
            v = (xv @ Wv.T).reshape(Bv, Tv, H, N).transpose(0, 2, 1, 3)
            g = jax.nn.gelu(xg @ Wg.T, approximate=False)
            w = jnp.exp(-jnp.exp(time_decay))[:, 0]
            u = time_faaaa[:, 0]
            q = jnp.arange(Q)
            ws = (w ** Q).reshape(1, H, 1, 1)
            wk = (w[:, None] ** (Q - 1 - q)).reshape(1, H, 1, Q)
            wb = (w[:, None] ** q).reshape(1, H, Q, 1)
            i_idx = q[:, None]
            j_idx = q[None, :]
            e = jnp.maximum(i_idx - j_idx - 1, 0)
            Wmat = jnp.where(i_idx > j_idx, w[:, None, None] ** e, 0.0)
            Wmat = Wmat + jnp.eye(Q, dtype=x.dtype) * u[:, None, None]
            Wmat = Wmat.reshape(1, H, Q, Q)
            rr = r.reshape(Bv, H, nC, Q, N).transpose(2, 0, 1, 3, 4)
            kk = k.reshape(Bv, H, N, nC, Q).transpose(3, 0, 1, 2, 4)
            vv = v.reshape(Bv, H, nC, Q, N).transpose(2, 0, 1, 3, 4)

            def step(state, inp):
                rc, kc, vc = inp
                att = rc @ kc
                yc = att * Wmat @ vc + rc @ state * wb
                new_state = ws * state + kc * wk @ vc
                return (new_state, yc)
            state0 = jnp.zeros((Bv, H, N, N), dtype=x.dtype)
            _, ys = jax.lax.scan(step, state0, (rr, kk, vv))
            y = ys.transpose(1, 2, 0, 3, 4).reshape(Bv, H, Tv, N)
            y = y.transpose(0, 2, 1, 3)
            mean = y.mean(axis=-1, keepdims=True)
            var = y.var(axis=-1, keepdims=True)
            yn = (y - mean) / jnp.sqrt(var + EPS)
            yn = yn * ln_w.reshape(1, 1, H, N) + ln_b.reshape(1, 1, H, N)
            yn = yn.reshape(Bv, Tv, C)
            out = yn * g @ Wo.T
            return out
        return _rwkv_forward(x, time_maa_k, time_maa_v, time_maa_r, time_maa_g, time_decay, time_faaaa, Wr, Wk, Wv, Wg, Wo, ln_w, ln_b)

    def _L0_ffn_ref(x, W_fc, ln_w, ln_b, W_proj):
        import jax, jax.numpy as jnp
        import numpy as np
        EPS = 1e-06
        LN_EPS = 1e-05

        def _absmean_core(W):
            gamma = jnp.mean(jnp.abs(W)) + EPS
            Ws = W / gamma
            Wq = jnp.sign(Ws) * jnp.minimum(jnp.round(jnp.abs(Ws)), 1.0)
            return (Wq, gamma)

        @jax.custom_vjp
        def absmean(W):
            return _absmean_core(W)[0]

        def _absmean_fwd(W):
            Wq, gamma = _absmean_core(W)
            return (Wq, gamma)

        def _absmean_bwd(gamma, g):
            return (g / gamma,)
        absmean.defvjp(_absmean_fwd, _absmean_bwd)

        def layernorm(x, w, b, eps=LN_EPS):
            mu = jnp.mean(x, axis=-1, keepdims=True)
            var = jnp.mean((x - mu) ** 2, axis=-1, keepdims=True)
            return (x - mu) * jax.lax.rsqrt(var + eps) * w + b
        h = jnp.einsum('btd,hd->bth', x, absmean(W_fc))
        h = jax.nn.gelu(h, approximate=False)
        h = layernorm(h, ln_w, ln_b)
        return jnp.einsum('bth,dh->btd', h, absmean(W_proj))
    x = x + _L0_xattn_ref(_layernorm(x, axis=-1), ctx_1024, ctx_1024, L0_xattn_Wq, L0_xattn_bq, L0_xattn_Wk, L0_xattn_bk, L0_xattn_Wv, L0_xattn_bv, L0_xattn_Wo, L0_xattn_bo)
    x = x + _L0_attn_ref(_layernorm(x, axis=-1), L0_attn_time_maa_k, L0_attn_time_maa_v, L0_attn_time_maa_r, L0_attn_time_maa_g, L0_attn_time_decay, L0_attn_time_faaaa, L0_attn_Wr, L0_attn_Wk, L0_attn_Wv, L0_attn_Wg, L0_attn_Wo, L0_attn_ln_w, L0_attn_ln_b)
    x = x + _L0_ffn_ref(_layernorm(x, axis=-1), L0_ffn_W_fc, L0_ffn_ln_w, L0_ffn_ln_b, L0_ffn_W_proj)
    return x

_drawn_inputs = setup_inputs


def setup_inputs(seed=0):
    import zlib

    import numpy as np

    out = dict(_drawn_inputs(seed))
    spreads = {'L0_xattn_bq': (0.0, 0.1),
     'L0_xattn_bk': (0.0, 2.0),
     'L0_xattn_bv': (0.0, 0.1),
     'L0_xattn_bo': (0.0, 0.1),
     'L0_attn_ln_w': (1.0, 0.6),
     'L0_attn_ln_b': (0.0, 0.8),
     'L0_ffn_ln_w': (1.0, 0.2),
     'L0_ffn_ln_b': (0.0, 0.1)}
    factors = {'L0_attn_time_maa_k': 8.0,
     'L0_attn_time_maa_v': 8.0,
     'L0_attn_time_maa_r': 8.0,
     'L0_attn_time_maa_g': 8.0,
     'L0_attn_time_decay': 64.0,
     'L0_attn_time_faaaa': 8.0,
     'L0_attn_Wr': 3.783,
     'L0_attn_Wk': 3.657,
     'L0_attn_Wv': 3.713,
     'L0_attn_Wg': 3.728,
     'L0_attn_Wo': 3.755}
    for name, (base, spread) in spreads.items():
        noise = np.random.default_rng([zlib.crc32(name.encode()), seed]).standard_normal(out[name].shape)
        drawn = base * np.exp(spread * noise) if base else spread * noise
        out[name] = jnp.asarray(drawn.astype(out[name].dtype))
    for name, factor in factors.items():
        out[name] = (out[name] * factor).astype(out[name].dtype)
    return out
```

```python
from contextlib import ExitStack

import numpy as np

import concourse.bass as bass
from concourse import mybir

F32 = mybir.dt.float32
F32R = mybir.dt.float32r
ALU = mybir.AluOpType
ACT = mybir.ActivationFunctionType
X = mybir.AxisListType.X

P = 128
B, T, D = 32, 64, 128
NT = B * T // P
H, DK = 16, 64
HP = H // 2
RH, RN = 16, 8
HG = 4
NGR = RH // HG
FH = 512
NK = FH // P
SCALE = DK ** -0.5
GT = 2
NG = NT // GT
GTOK = GT * P
CT = 4
NC = NT // CT
CTOK = CT * P
LN_EPS = 1e-5
GN_EPS = 1e-5 * 64
GAMMA_EPS = 1e-6
MASKED = -3.0e38
DECAY_CAP = 1e30

COL_BQ, COL_BK, COL_MAA, COL_GNW, COL_GNB, COL_LNW, COL_LNB, NCOL = 0, 8, 16, 20, 21, 22, 26, 30
C_ID, C_CEN, C_AVG, C_ONES, C_CAUSAL, C_EXP, C_LOWER, C_DIAG, C_HEADM, NCONST = (
    0, 128, 256, 384, 512, 576, 640, 704, 768, 772)


def shape_constants():
    c = np.zeros((P, NCONST), np.float32)
    i = np.arange(P)
    t = np.arange(T)
    same = (i[:, None] // RN == i[None, :] // RN).astype(np.float32) / RN
    c[:, C_ID:C_CEN] = np.eye(P)
    c[:, C_CEN:C_AVG] = np.eye(P) - same
    c[:, C_AVG:C_ONES] = same
    c[:, C_ONES:C_CAUSAL] = 1.0 / (FH * D)
    c[:, C_CAUSAL:C_EXP] = np.where(t[None, :] > (i % T)[:, None], MASKED, 0.0)
    c[:, C_EXP:C_LOWER] = np.maximum(t[None, :] - (i % T)[:, None] - 1, 0)
    c[:, C_LOWER:C_DIAG] = t[None, :] > (i % T)[:, None]
    c[:, C_DIAG:C_HEADM] = t[None, :] == (i % T)[:, None]
    c[:, C_HEADM:] = (i[:, None] // RN) % HG == np.arange(HG)[None, :]
    return c


class Ticket:

    def __init__(self, sem, value):
        self.sem, self.value = sem, value


class Queue:

    def __init__(self, name, new_sem):
        self.name, self.new_sem = name, new_sem
        self.steps, self.sems, self.counts, self.seen = [], {}, {}, {}

    def after(self, *tickets):
        for t in tickets:
            if t is not None and self.seen.get(id(t.sem), 0) < t.value:
                self.seen[id(t.sem)] = t.value
                self.steps.append(("wait", t.sem, t.value))

    def do(self, build, stage=None, by=1):
        if stage is None:
            self.steps.append(("run", build, None, 0))
            return None
        if stage not in self.sems:
            self.sems[stage] = self.new_sem(f"{self.name}_{stage}")
            self.counts[stage] = 0
        self.counts[stage] += by
        self.steps.append(("run", build, self.sems[stage], by))
        return Ticket(self.sems[stage], self.counts[stage])

    def play(self, engine):
        for s in self.steps:
            if s[0] == "wait":
                engine.wait_ge(s[1], s[2])
            else:
                made = s[1](engine)
                if s[2] is not None:
                    made.then_inc(s[2], s[3])


def build_block(nc, x, ctxT, w_q, w_k, w_v, w_o, rows, dec_u, cols, w_rwkv, w_fc, w_proj, consts, out):
    with ExitStack() as stack:
        def sb(name, shape, dt=F32):
            return stack.enter_context(nc.sbuf_tensor(name, shape, dt))

        def new_sem(name):
            return stack.enter_context(nc.semaphore(name))

        pe, act, dve, pool, sp = (Queue(n, new_sem) for n in ("pe", "act", "dve", "pool", "sp"))

        const = sb("const", [P, NCONST])
        col = sb("col", [P, NCOL])
        x_tok = sb("x_tok", [P, NT, D])
        ln_stat = sb("ln_stat", [P, NT, 6])
        ln_mv = sb("ln_mv", [P, NT, 2])
        ln_rstd = sb("ln_rstd", [P, NT])
        gamma = sb("gamma", [P, 8])
        w_raw = sb("w_raw", [P, 3, H * DK])
        wo_sb = sb("wo_sb", [P, HP, D])
        bo_bc = sb("bo_bc", [P, D])
        bv_bc = sb("bv_bc", [P, H * DK])
        decu_bc = sb("decu_bc", [P, 2 * RH])
        wrk = sb("wrk", [P, 5, D])
        w_hi = sb("w_hi", [P, 3, H * DK], F32R)
        w_lo = sb("w_lo", [P, 3, H * DK], F32R)
        xT_hi = sb("xT_hi", [P, B * T], F32R)
        xT_lo = sb("xT_lo", [P, B * T], F32R)
        wfc_t = sb("wfc_t", [P, FH], F32R)
        wpr_t = sb("wpr_t", [P, NK, D])
        wfc_raw = sb("wfc_raw", [P, FH])
        wpr_raw = sb("wpr_raw", [P, NK * D])
        wmatT = sb("wmatT", [P, RH, T])

        cT_hi = sb("cT_hi", [P, B * T], F32R)
        cT_lo = sb("cT_lo", [P, B * T], F32R)
        arena = sb("arena", [P, 25 * 1024])
        used = [0]

        def cut(n):
            a = arena[:, used[0]:used[0] + n]
            used[0] += n
            assert used[0] <= 25 * 1024
            return a

        cT = cut(B * T)
        used[0] = 0
        q_sb = [cut(HP * GTOK).rearrange("p (c t) -> p c t", c=HP) for _ in range(2)]
        k_sb = [cut(HP * GTOK).rearrange("p (c t) -> p c t", c=HP) for _ in range(2)]
        v_sb = [cut(GT * H * DK).rearrange("p (g n) -> p g n", g=GT) for _ in range(2)]
        s_sb = [cut(2 * HP * T).rearrange("p (c b k) -> p c b k", c=HP, b=2) for _ in range(2)]
        e_sb = [cut(2 * HP * T).rearrange("p (c b k) -> p c b k", c=HP, b=2) for _ in range(2)]
        pT_sb = [cut(HP * P).rearrange("p (c q) -> p c q", c=HP) for _ in range(2)]
        o_sb = [cut(HP * P).rearrange("p (c q) -> p c q", c=HP) for _ in range(2)]
        s_max = [cut(2 * HP).rearrange("p (c b) -> p c b", c=HP) for _ in range(2)]
        s_sum = [cut(2 * HP).rearrange("p (c b) -> p c b", c=HP) for _ in range(2)]
        s_rec = [cut(2 * HP).rearrange("p (c b) -> p c b", c=HP) for _ in range(2)]
        xn_tok = w_raw[:, 0:2, :].rearrange("p a n -> p (a n)").rearrange("p (t d) -> p t d", t=NT)
        ln1_tok = arena[:, 12 * 1024:14 * 1024].rearrange("p (t d) -> p t d", t=NT)

        bank = [stack.enter_context(nc.psum_tensor(f"bank{i}", [P, 512], F32)) for i in range(8)]

        ident = const[:, C_ID:C_ID + P]
        centre = const[:, C_CEN:C_CEN + P]
        average = const[:, C_AVG:C_AVG + P]

        def load(queue, name, dst, src):
            return queue.do(lambda e: e.dma_start(dst, src), f"load_{name}", 16)

        ld_x = [load(sp, f"x{c}", x_tok[:, c * CT:(c + 1) * CT, :].rearrange("p t d -> p (t d)"),
                     x[:, c * CTOK:(c + 1) * CTOK]) for c in range(NC)]
        ld_w = [load(act, n, w_raw[:, i, :], w) for i, (n, w) in enumerate((("wq", w_q), ("wk", w_k), ("wv", w_v)))]
        ld_const = load(sp, "const", const[:, :], consts)
        ld_c = load(sp, "ctx", cT, ctxT)
        ld_col = load(act, "col", col[:, :], cols)
        ld_bv = load(sp, "bv", bv_bc[:, :], rows[0:1, 0:H * DK].to_broadcast([P, H * DK]))
        ld_bo = load(sp, "bo", bo_bc[:, :], rows[0:1, H * DK:].to_broadcast([P, D]))
        ld_wo = load(sp, "wo", wo_sb[:, :, :].rearrange("p c n -> p (c n)"), w_o)
        ld_decu = load(sp, "decu", decu_bc[:, :], dec_u[0:1, :].to_broadcast([P, 2 * RH]))
        ld_wrk = load(sp, "wrk", wrk[:, :, :].rearrange("p a n -> p (a n)"), w_rwkv)
        ld_fc = load(sp, "fc", wfc_raw[:, :], w_fc)
        ld_proj = load(sp, "proj", wpr_raw[:, :], w_proj)

        def ln_stats(t, ready):
            dve.after(ready)
            s = dve.do(lambda e: e.bn_stats(ln_stat[:, t, :], x_tok[:, t, :]), "ln_stats")
            return s

        def ln_aggr(t, stats):
            dve.after(stats)
            return dve.do(lambda e: e.bn_aggr(ln_mv[:, t, :], ln_stat[:, t, :]), "ln_aggr")

        def ln_rstd_of(t0, t1, aggr):
            dve.after(aggr)
            add = dve.do(lambda e: e.tensor_scalar(ln_rstd[:, t0:t1], ln_mv[:, t0:t1, 1], LN_EPS, None, ALU.add),
                         "ln_eps")
            act.after(add)
            root = act.do(lambda e: e.activation(ln_rstd[:, t0:t1], ln_rstd[:, t0:t1], ACT.Sqrt), "ln_sqrt")
            dve.after(root)
            return dve.do(lambda e: e.reciprocal(ln_rstd[:, t0:t1], ln_rstd[:, t0:t1]), "ln_rstd")

        def ln_apply(t, dst, rstd):
            dve.after(rstd)
            return dve.do(lambda e: e.tensor_scalar(dst, x_tok[:, t, :], ln_mv[:, t, 0:1], ln_rstd[:, t:t + 1],
                                                    ALU.subtract, ALU.mult), "ln_apply")

        def layer_norm(tiles, dst, ready):
            stats = [ln_stats(t, r) for t, r in zip(tiles, ready)]
            for t, s in zip(tiles, stats):
                aggr = ln_aggr(t, s)
            rstd = ln_rstd_of(tiles[0], tiles[-1] + 1, aggr)
            for t in tiles:
                done = ln_apply(t, dst[:, t, :], rstd)
            return done

        def transpose_tiles(psum, src, tiles, ready, stage):
            pe.after(ld_const, *ready)
            for j, t in enumerate(tiles):
                done = pe.do(lambda e, j=j, t=t: e.transpose(psum[:, j * P:(j + 1) * P], src[:, t, :], ident),
                             stage if j == len(tiles) - 1 else None)
            return done

        def split(raw, hi, lo, ready):
            act.after(ready)
            rounded = act.do(lambda e: e.activation(hi, raw, ACT.Copy), "split_hi")
            pool.after(rounded)
            return pool.do(lambda e: e.tensor_tensor(lo, raw, hi.bitcast(F32), ALU.subtract), "split_lo")

        chunk = lambda c: range(c * CT, (c + 1) * CT)
        w_split, xT_split, c_split = [None] * 3, [None] * NC, [None] * NC

        def split_x(c, psum, transposed, stage):
            sl = slice(c * CTOK, (c + 1) * CTOK)
            act.after(transposed)
            hi = act.do(lambda e: e.activation(xT_hi[:, sl], psum[:, :], ACT.Copy), stage + "_hi")
            dve.after(hi)
            return dve.do(lambda e: e.tensor_tensor(xT_lo[:, sl], psum[:, :], xT_hi[:, sl].bitcast(F32),
                                                    ALU.subtract), stage + "_lo")

        def split_ctx(c):
            sl = slice(c * CTOK, (c + 1) * CTOK)
            c_split[c] = split(cT[:, sl], cT_hi[:, sl], cT_lo[:, sl], ld_c)

        def split_w(i):
            w_split[i] = split(w_raw[:, i, :], w_hi[:, i, :], w_lo[:, i, :], ld_w[i])

        split_w(0)
        split_w(1)
        for c in range(NC):
            split_ctx(c)
            normed = layer_norm(chunk(c), ln1_tok, [ld_x[c]] * CT)
            turned = transpose_tiles(bank[c], ln1_tok, chunk(c), [normed], "turn_x")
            xT_split[c] = split_x(c, bank[c], turned, "split_x")
        split_w(2)
        prologue_done = (xT_split[-1], c_split[-1])

        pool.after(ld_bo, normed)
        add_bo = pool.do(lambda e: e.tensor_tensor(
            x_tok[:, :, :], x_tok[:, :, :], bo_bc[:, :].unsqueeze(1).to_broadcast([P, NT, D]), ALU.add), "add_bo")

        def build_decay():
            act.after(ld_decu, ld_const)
            a = act.do(lambda e: e.activation(decu_bc[:, 0:RH], decu_bc[:, 0:RH], ACT.Exp), "decay")
            pool.after(a)
            b = pool.do(lambda e: e.tensor_scalar(decu_bc[:, 0:RH], decu_bc[:, 0:RH], DECAY_CAP, -1.0, ALU.min,
                                                  ALU.mult), "decay")
            act.after(b)
            for h in range(RH):
                a = act.do(lambda e, h=h: e.activation(wmatT[:, h, :], const[:, C_EXP:C_EXP + T], ACT.Exp,
                                                       scale=decu_bc[:, h:h + 1]), "decay")
            heads = lambda c: const[:, c:c + T].unsqueeze(1).to_broadcast([P, RH, T])
            tmp = w_raw[:, 2, :].rearrange("p (h i) -> p h i", h=RH)
            pool.after(a)
            lower = pool.do(lambda e: e.tensor_tensor(wmatT[:, :, :], wmatT[:, :, :], heads(C_LOWER), ALU.mult),
                            "decay_lower")
            pool.after(w_split[2])
            diag = pool.do(lambda e: e.tensor_tensor(
                tmp, heads(C_DIAG), decu_bc[:, RH:2 * RH].unsqueeze(2).to_broadcast([P, RH, T]), ALU.mult),
                "decay_diag")
            pool.after(lower, diag)
            return pool.do(lambda e: e.tensor_tensor(wmatT[:, :, :], wmatT[:, :, :], tmp, ALU.add), "decay_sum")

        def build_ternary(raw, dst, ready, psum, psum_free, g, name):
            scratch = w_raw[:, 2, 0:FH]
            act.after(ready, decay_ready)
            total = act.do(lambda e: e.activation(scratch, raw, ACT.Abs, accum_out=gamma[:, g:g + 1]), name + "_abs")
            pe.after(total, ld_const, psum_free)
            mean = pe.do(lambda e: e.matmul(psum[:, 0:1], const[:, C_ONES:C_ONES + P], gamma[:, g:g + 1],
                                            start=True, stop=True), name + "_mean")
            dve.after(mean)
            up = dve.do(lambda e: e.tensor_scalar(gamma[:, g + 1:g + 2], psum[:, 0:1], GAMMA_EPS, 0.5, ALU.add,
                                                  ALU.mult), name + "_thr")
            down = dve.do(lambda e: e.tensor_scalar(gamma[:, g + 2:g + 3], psum[:, 0:1], GAMMA_EPS, -0.5, ALU.add,
                                                    ALU.mult), name + "_thr")
            dve.after(up, down)
            below = dve.do(lambda e: e.tensor_scalar(scratch, raw, gamma[:, g + 2:g + 3], None, ALU.is_lt),
                           name + "_below")
            dve.after(below)
            return mean, dve.do(lambda e: e.scalar_tensor_tensor(
                out=dst, in0=raw, scalar=gamma[:, g + 1:g + 2], in1=scratch, op0=ALU.is_gt, op1=ALU.subtract),
                name + "_ternary")

        PROJ = (0, 1)
        S_BANK, PT_BANK, O_BANK = (2, 3), (4, 5), (6, 7)
        proj_read = [None, None]
        proj_turn = [0]
        q_done, k_done, v_done = ([None] * NG for _ in range(3))
        q_used, k_used, v_used = ([None] * NG for _ in range(3))
        s_mm, s_masked, p_norm, pT_done, pv_mm, o_done, wo_mm, res_done = ([None] * NT for _ in range(8))
        exp_done, turned_p = [None] * NT, [None] * NT

        def next_proj_bank():
            i = proj_turn[0] % 2
            proj_turn[0] += 1
            pe.after(proj_read[i], *(prologue_done if proj_turn[0] <= 2 else ()))
            return i

        def project_qk(g, which, c):
            i = next_proj_bank()
            hi, lo = (xT_hi, xT_lo) if which == 0 else (cT_hi, cT_lo)
            tok = slice(g * GTOK, (g + 1) * GTOK)
            pe.after(w_split[which], (xT_split if which == 0 else c_split)[g * GTOK // CTOK])
            for j in range(2):
                w = slice((2 * c + j) * P, (2 * c + j + 1) * P)
                o = bank[PROJ[i]][:, j * GTOK:(j + 1) * GTOK]
                pe.do(lambda e, w=w, o=o: e.matmul(o, w_hi[:, which, w], lo[:, tok], start=True, stop=False))
                pe.do(lambda e, w=w, o=o: e.matmul(o, w_lo[:, which, w], hi[:, tok], start=False, stop=False))
                mm = pe.do(lambda e, w=w, o=o: e.matmul(o, w_hi[:, which, w], hi[:, tok], start=False, stop=True),
                           "project" if j else None)
            dst = (q_sb, k_sb)[which][g % 2]
            bias = (COL_BQ, COL_BK)[which]
            act.after(mm, ld_col, (q_used, k_used)[which][g - 2] if g >= 2 else None)
            for j in range(2):
                done = act.do(lambda e, j=j: e.activation(
                    dst[:, 2 * c + j, :], bank[PROJ[i]][:, j * GTOK:(j + 1) * GTOK], ACT.Identity,
                    bias=col[:, bias + 2 * c + j:bias + 2 * c + j + 1]), "project" if j else None)
            proj_read[i] = done
            (q_done, k_done)[which][g] = done

        def project_v(g, n):
            tt, half = n // 2, n % 2
            i = next_proj_bank()
            tok = slice((g * GT + tt) * P, (g * GT + tt + 1) * P)
            w = slice(half * 512, half * 512 + 512)
            pe.after(w_split[2], c_split[g * GTOK // CTOK])
            o = bank[PROJ[i]][:, :]
            pe.do(lambda e: e.matmul(o, cT_lo[:, tok], w_hi[:, 2, w], start=True, stop=False))
            pe.do(lambda e: e.matmul(o, cT_hi[:, tok], w_lo[:, 2, w], start=False, stop=False))
            mm = pe.do(lambda e: e.matmul(o, cT_hi[:, tok], w_hi[:, 2, w], start=False, stop=True), "project")
            dve.after(mm, ld_bv, v_used[g - 2] if g >= 2 else None)
            v_done[g] = proj_read[i] = dve.do(lambda e: e.tensor_tensor(
                v_sb[g % 2][:, tt, w], o, bv_bc[:, w], ALU.add), "project")

        def scores(t):
            g, tt = t // GT, t % GT
            pe.after(q_done[g], k_done[g], s_masked[t - 1] if t >= 1 else None)
            for c in range(HP):
                for par, b in ((0, 0), (1, 1), (0, 1), (1, 0)):
                    rows_ = slice(par * DK, par * DK + DK)
                    tok = slice(tt * P + b * T, tt * P + b * T + T)
                    mm = pe.do(lambda e, c=c, b=b, rows_=rows_, tok=tok: e.matmul(
                        bank[S_BANK[b]][rows_, c * T:(c + 1) * T], q_sb[g % 2][rows_, c, tok],
                        k_sb[g % 2][rows_, c, tok], start=True, stop=True),
                        "scores" if (c, par, b) == (HP - 1, 1, 0) else None)
            s_mm[t] = mm
            if tt == GT - 1:
                q_used[g] = k_used[g] = mm

        def softmax(t):
            r = t % 2
            dve.after(s_mm[t], exp_done[t - 2] if t >= 2 else None)
            causal = const[:, C_CAUSAL:C_CAUSAL + T].unsqueeze(1).to_broadcast([P, HP, T])
            for b in range(2):
                s_masked[t] = dve.do(lambda e, b=b: e.tensor_tensor(
                    s_sb[r][:, :, b, :], bank[S_BANK[b]][:, :].rearrange("p (c k) -> p c k", c=HP), causal,
                    ALU.add), "mask")
            dve.after(s_masked[t])
            top = dve.do(lambda e: e.tensor_reduce(s_max[r], s_sb[r], X, ALU.max), "max")
            pool.after(top)
            less = pool.do(lambda e: e.tensor_tensor(
                s_sb[r], s_sb[r], s_max[r].unsqueeze(3).to_broadcast([P, HP, 2, T]), ALU.subtract), "less_max")
            act.after(less, turned_p[t - 2] if t >= 2 else None)
            exp_done[t] = act.do(lambda e: e.activation(e_sb[r], s_sb[r], ACT.Exp, scale=SCALE), "exp")
            dve.after(exp_done[t])
            total = dve.do(lambda e: e.tensor_reduce(s_sum[r], e_sb[r], X, ALU.add), "sum")
            dve.after(total)
            rec = dve.do(lambda e: e.reciprocal(s_rec[r], s_sum[r]), "rec")
            pool.after(rec)
            p_norm[t] = pool.do(lambda e: e.tensor_tensor(
                e_sb[r], e_sb[r], s_rec[r].unsqueeze(3).to_broadcast([P, HP, 2, T]), ALU.mult), "normalise")

        def turn_probs(t):
            pe.after(p_norm[t], pT_done[t - 1] if t >= 1 else None)
            for c in range(HP):
                mm = pe.do(lambda e, c=c: e.transpose(
                    bank[PT_BANK[c // 4]][:, (c % 4) * P:(c % 4 + 1) * P],
                    e_sb[t % 2][:, c, :, :].rearrange("p b k -> p (b k)"), ident),
                    "turn_p" if c % 4 == 3 else None)
                if c % 4 == 3:
                    act.after(mm, pv_mm[t - 2] if t >= 2 else None)
                    done = act.do(lambda e, c=c: e.activation(
                        pT_sb[t % 2][:, c - 3:c + 1, :].rearrange("p c q -> p (c q)"), bank[PT_BANK[c // 4]][:, :],
                        ACT.Copy), "turn_p")
            turned_p[t], pT_done[t] = mm, done

        def values(t):
            g, tt = t // GT, t % GT
            pe.after(pT_done[t], v_done[g], o_done[t - 1] if t >= 1 else None)
            for c in range(HP):
                for b, par in ((0, 0), (1, 1), (0, 1), (1, 0)):
                    keys = slice(b * T, b * T + T)
                    h = 2 * c + par
                    mm = pe.do(lambda e, c=c, b=b, par=par, keys=keys, h=h: e.matmul(
                        bank[O_BANK[b]][par * DK:par * DK + DK, c * T:(c + 1) * T],
                        v_sb[g % 2][keys, tt, h * DK:(h + 1) * DK], pT_sb[t % 2][keys, c, par * T:par * T + T],
                        start=True, stop=True), "values" if (c, b, par) == (HP - 1, 1, 0) else None)
            pv_mm[t] = mm
            if tt == GT - 1:
                v_used[g] = mm
            for b in range(2):
                dve.after(mm, wo_mm[t - 2] if t >= 2 else None)
                o_done[t] = dve.do(lambda e, b=b: e.tensor_copy(
                    o_sb[t % 2][:, :, b * T:(b + 1) * T], bank[O_BANK[b]][:, :].rearrange("p (c q) -> p c q", c=HP)),
                    "values")

        def output(t):
            i = next_proj_bank()
            pe.after(o_done[t], ld_wo)
            for c in range(HP):
                mm = pe.do(lambda e, c=c: e.matmul(bank[PROJ[i]][:, 0:D], o_sb[t % 2][:, c, :], wo_sb[:, c, :],
                                                   start=(c == 0), stop=(c == HP - 1)),
                           "output" if c == HP - 1 else None)
            wo_mm[t] = mm
            dve.after(mm, add_bo)
            proj_read[i] = res_done[t] = dve.do(lambda e: e.tensor_tensor(
                x_tok[:, t, :], bank[PROJ[i]][:, 0:D], x_tok[:, t, :], ALU.add), "output")

        jobs = []
        for g in range(NG):
            jobs += [lambda g=g, c=c: project_qk(g, 0, c) for c in range(HP // 2)]
            jobs += [lambda g=g, c=c: project_qk(g, 1, c) for c in range(HP // 2)]
            jobs += [lambda g=g, n=n: project_v(g, n) for n in range(2 * GT)]

        def run_jobs(n):
            for _ in range(min(n, len(jobs))):
                jobs.pop(0)()

        run_jobs(8)
        scores(0)
        softmax(0)
        run_jobs(4)
        scores(1)
        softmax(1)
        run_jobs(6)
        for t in range(NT):
            turn_probs(t)
            run_jobs(2)
            if t >= 1:
                output(t - 1)
            values(t)
            run_jobs(4)
            if t + 2 < NT:
                scores(t + 2)
                softmax(t + 2)
        output(NT - 1)

        attention_left = (wo_mm[-1], res_done[-1], p_norm[-1], pT_done[-1])
        for queue in (pe, act, dve, pool):
            queue.after(*attention_left)

        decay_ready = build_decay()
        mean1, fc_ready = build_ternary(wfc_raw[:, :], wfc_t[:, :], ld_fc, bank[6], None, 0, "fc")
        act.after(fc_ready)
        mean2, proj_ready = build_ternary(wpr_raw[:, :], wpr_t[:, :, :].rearrange("p k n -> p (k n)"), ld_proj,
                                          bank[7], None, 3, "proj")

        used[0] = 0
        SEQ = T + 1
        xs = cut(B * SEQ).rearrange("p (b t) -> p b t", b=B)
        xx = cut(B * T).rearrange("p (b t) -> p b t", b=B)
        mixed = [cut(4 * CTOK).rearrange("p (m n) -> p m n", m=4) for _ in range(2)]
        r_exp = [cut(HG * CTOK).rearrange("p (m b i) -> p b m i", m=HG, i=T) for _ in range(2)]
        kT = [cut(CTOK) for _ in range(2)]
        v_tok = [cut(CTOK).rearrange("p (t d) -> p t d", t=CT) for _ in range(2)]
        g_sb = cut(B * T)
        attw = [cut(2 * RH * T).rearrange("p (g s n) -> p g s n", g=NGR, s=2) for _ in range(2)]
        yT = cut(B * T)
        sq, sd, nrm, zT = (cut(CTOK) for _ in range(4))

        pool_zero = pool.do(lambda e: e.memset(xs[:, :, 0:1], 0.0), "zero")
        A_BANK, Y_BANK, M_BANK = (0, 1, 2, 3), (4, 5), (6, 7)
        misc_read, misc_turn = [proj_ready, proj_ready], [0]

        def misc_bank():
            i = misc_turn[0] % 2
            misc_turn[0] += 1
            pe.after(misc_read[i])
            return i, bank[M_BANK[i]]

        xs_done, mix_done, g_done = [None] * NC, [None] * NC, [None] * NC
        r_done, k_done2, v_done2 = [None] * NC, [None] * NC, [None] * NC
        NB = CTOK // T
        for c in range(NC):
            normed = layer_norm(chunk(c), xn_tok, [res_done[-1]] * CT)
            i, psum = misc_bank()
            turned = transpose_tiles(psum, xn_tok, chunk(c), [normed], "turn_x2")
            act.after(turned)
            misc_read[i] = xs_done[c] = act.do(lambda e, c=c, psum=psum: e.activation(
                xs[:, c * NB:(c + 1) * NB, 1:], psum[:, :].rearrange("p (b t) -> p b t", t=T), ACT.Copy), "xs")

        proj_mm = {}

        def mix(c):
            bs = slice(c * NB, (c + 1) * NB)
            pool.after(xs_done[c], pool_zero)
            diff = pool.do(lambda e: e.tensor_tensor(xx[:, bs, :], xs[:, bs, 0:T], xs[:, bs, 1:], ALU.subtract), "xx")
            dve.after(diff, ld_col, proj_mm.get(c - 2))
            for m in range(4):
                mix_done[c] = dve.do(lambda e, m=m: e.scalar_tensor_tensor(
                    out=mixed[c % 2][:, m, :].rearrange("p (b t) -> p b t", t=T), in0=xx[:, bs, :],
                    scalar=col[:, COL_MAA + m:COL_MAA + m + 1], in1=xs[:, bs, 1:], op0=ALU.mult, op1=ALU.add), "mix")

        def project_rwkv(c):
            ready = (mix_done[c], ld_wrk)
            src = mixed[c % 2]
            i, psum = misc_bank()
            pe.after(*ready)
            mm = pe.do(lambda e, psum=psum: e.matmul(psum[:, :], wrk[:, 3, :], src[:, 3, :], start=True, stop=True),
                       "rwkv")
            act.after(mm)
            misc_read[i] = g_done[c] = act.do(lambda e, psum=psum: e.activation(
                g_sb[:, c * CTOK:(c + 1) * CTOK], psum[:, :], ACT.Gelu), "gate")
            i, psum = misc_bank()
            mm = pe.do(lambda e, psum=psum: e.matmul(psum[:, :], wrk[:, 1, :], src[:, 0, :], start=True, stop=True),
                       "rwkv")
            dve.after(mm, att_mm[2 * c - 3] if c >= 2 else None)
            misc_read[i] = k_done2[c] = dve.do(lambda e, psum=psum: e.tensor_copy(kT[c % 2], psum[:, :]), "k")
            i, psum = misc_bank()
            mm = pe.do(lambda e, psum=psum: e.matmul(psum[:, :], wrk[:, 0, :], src[:, 2, :], start=True, stop=True),
                       "rwkv")
            act.after(mm, att_mm[2 * c - 3] if c >= 2 else None)
            for m in range(HG):
                r_done[c] = act.do(lambda e, m=m, psum=psum: e.activation(
                    r_exp[c % 2][:, :, m, :], psum[:, :].rearrange("p (b i) -> p b i", i=T), ACT.Copy,
                    scale=const[:, C_HEADM + m:C_HEADM + m + 1]), "r")
            misc_read[i] = r_done[c]
            i, psum = misc_bank()
            for t in range(CT):
                mm = pe.do(lambda e, t=t, psum=psum: e.matmul(
                    psum[:, t * D:(t + 1) * D], src[:, 1, t * P:(t + 1) * P], wrk[:, 2, :], start=True, stop=True),
                    "rwkv" if t == CT - 1 else None)
            proj_mm[c] = mm
            dve.after(mm, y_mm[2 * c - 3] if c >= 2 else None)
            misc_read[i] = v_done2[c] = dve.do(lambda e, psum=psum: e.tensor_copy(
                v_tok[c % 2].rearrange("p t d -> p (t d)"), psum[:, :]), "v")

        NS = NT // 2
        att_mm, attw_done, y_mm, y_done = [None] * NS, [None] * NS, [None] * NS, [None] * NS
        att_read = [None] * 4

        def attend(s):
            c, base = s // 2, (s % 2) * 4
            pe.after(r_done[c], k_done2[c], *att_read)
            for tt in range(2):
                for par in range(2):
                    b = base + 2 * tt + par
                    for n in range(NGR):
                        ch = slice(32 * n, 32 * n + 32)
                        mm = pe.do(lambda e, tt=tt, par=par, b=b, n=n, ch=ch: e.matmul(
                            bank[A_BANK[n]][par * T:par * T + T, tt * HG * T:(tt + 1) * HG * T],
                            kT[c % 2][ch, b * T:(b + 1) * T],
                            r_exp[c % 2][ch, b, :, :],
                            start=True, stop=True, tile_position=(32 * n, par * T)),
                            "attend" if (tt, par, n) == (1, 1, NGR - 1) else None)
            att_mm[s] = mm
            dve.after(mm, decay_ready, y_mm[s - 2] if s >= 2 else None)
            for n in range(NGR):
                att_read[n] = attw_done[s] = dve.do(lambda e, n=n: e.tensor_tensor(
                    attw[s % 2][:, n, :, :], bank[A_BANK[n]][:, :].rearrange("p (s n) -> p s n", s=2),
                    wmatT[:, HG * n:HG * n + HG, :].rearrange("p h i -> p (h i)").unsqueeze(1)
                    .to_broadcast([P, 2, HG * T]), ALU.mult), "decayed")

        def mix_values(s):
            c, tb = s // 2, (s % 2) * 2
            pe.after(attw_done[s], v_done2[c], y_done[s - 1] if s >= 1 else None)
            for tt in range(2):
                for n in range(NGR):
                    for par in range(2):
                        mm = pe.do(lambda e, tt=tt, par=par, n=n: e.matmul(
                            bank[Y_BANK[par]][32 * n:32 * n + 32, tt * HG * T:(tt + 1) * HG * T],
                            v_tok[c % 2][par * T:par * T + T, tb + tt, 32 * n:32 * n + 32],
                            attw[s % 2][par * T:par * T + T, n, tt, :], start=True, stop=True,
                            tile_position=(par * T, 32 * n)),
                            "mix_values" if (tt, n, par) == (1, NGR - 1, 1) else None)
            y_mm[s] = mm
            y_view = yT.rearrange("p (s t b i) -> p s t b i", s=NS, t=2, b=2)
            last = [mm, mm]
            for m in range(HG):
                for par in range(2):
                    src = bank[Y_BANK[par]][:, :].rearrange("p (t m i) -> p t m i", t=2, m=HG)[:, :, m, :]
                    dst = y_view[:, s, :, par, :]
                    mask = const[:, C_HEADM + m:C_HEADM + m + 1]
                    dve.after(last[par])
                    if m == 0:
                        last[par] = dve.do(lambda e, src=src, dst=dst, mask=mask: e.tensor_scalar(
                            dst, src, mask, None, ALU.mult), "own_head")
                    else:
                        last[par] = dve.do(lambda e, src=src, dst=dst, mask=mask: e.scalar_tensor_tensor(
                            out=dst, in0=src, scalar=mask, in1=dst, op0=ALU.mult, op1=ALU.add), "own_head")
            y_done[s] = last[1]

        for c in range(NC):
            if c == 0:
                mix(0)
                mix(1)
            project_rwkv(c)
            if c + 2 < NC:
                mix(c + 2)
            attend(2 * c)
            if c > 0:
                mix_values(2 * c - 1)
            attend(2 * c + 1)
            mix_values(2 * c)
        mix_values(NS - 1)

        z_mm, rwkv_done = [None] * NC, [None] * NC

        def finish_rwkv(c):
            sl = slice(c * CTOK, (c + 1) * CTOK)
            cen, var, zo = bank[2 * (c % 2)], bank[2 * (c % 2) + 1], bank[4 + c % 2]
            pe.after(y_done[2 * c + 1], attw_done[NS - 1], y_done[NS - 1], rwkv_done[c - 2] if c >= 2 else None)
            mm = pe.do(lambda e: e.matmul(cen[:, :], centre, yT[:, sl], start=True, stop=True), "centre")
            prev = z_mm[c - 1] if c >= 1 else None
            act.after(mm, prev)
            squared = act.do(lambda e: e.activation(sq, cen[:, :], ACT.Square), "square")
            pe.after(squared)
            mm = pe.do(lambda e: e.matmul(var[:, :], average, sq, start=True, stop=True), "variance")
            dve.after(mm, prev)
            eps = dve.do(lambda e: e.tensor_scalar(sd, var[:, :], GN_EPS, None, ALU.add), "gn_eps")
            act.after(eps)
            root = act.do(lambda e: e.activation(sd, sd, ACT.Sqrt), "gn_sqrt")
            dve.after(root)
            rec = dve.do(lambda e: e.reciprocal(sd, sd), "gn_rec")
            dve.after(rec)
            n1 = dve.do(lambda e: e.tensor_tensor(nrm, cen[:, :], sd, ALU.mult), "gn")
            dve.after(n1)
            n2 = dve.do(lambda e: e.tensor_scalar(nrm, nrm, col[:, COL_GNW:COL_GNW + 1], col[:, COL_GNB:COL_GNB + 1],
                                                  ALU.mult, ALU.add), "gn_affine")
            dve.after(n2, g_done[c])
            gated = dve.do(lambda e: e.tensor_tensor(zT, nrm, g_sb[:, sl], ALU.mult), "gated")
            pe.after(gated)
            for t in range(CT):
                mm = pe.do(lambda e, t=t: e.matmul(zo[:, t * D:(t + 1) * D], zT[:, t * P:(t + 1) * P], wrk[:, 4, :],
                                                   start=True, stop=True), "rwkv_out" if t == CT - 1 else None)
            z_mm[c] = mm
            dve.after(mm)
            rwkv_done[c] = dve.do(lambda e: e.tensor_tensor(
                x_tok[:, c * CT:(c + 1) * CT, :].rearrange("p t d -> p (t d)"),
                x_tok[:, c * CT:(c + 1) * CT, :].rearrange("p t d -> p (t d)"), zo[:, :], ALU.add), "rwkv_res")

        for c in range(NC):
            finish_rwkv(c)

        for queue in (pe, act, dve, pool):
            queue.after(rwkv_done[-1])
        used[0] = 0
        h_tok = cut(NT * FH).rearrange("p (t n) -> p t n", t=NT)
        hT = [cut(NK * CTOK).rearrange("p (k n) -> p k n", k=NK) for _ in range(2)]
        h_stat = cut(NT * 6).rearrange("p (t n) -> p t n", t=NT)
        h_mv = cut(NT * 2).rearrange("p (t n) -> p t n", t=NT)
        h_rstd = cut(NT)
        x3_split = [None] * NC
        for c in range(NC):
            normed = layer_norm(chunk(c), xn_tok, [rwkv_done[c]] * CT)
            turned = transpose_tiles(bank[c], xn_tok, chunk(c), [normed], "turn_x3")
            x3_split[c] = split_x(c, bank[c], turned, "split_x3")
        h_read, h_aggr = [None] * 4, [None] * NT
        for t in range(NT):
            psum = bank[4 + t % 4]
            tok = slice(t * P, (t + 1) * P)
            pe.after(x3_split[t // CT], fc_ready, h_read[t % 4])
            pe.do(lambda e, psum=psum, tok=tok: e.matmul(psum[:, :], xT_lo[:, tok], wfc_t[:, :], start=True,
                                                         stop=False))
            mm = pe.do(lambda e, psum=psum, tok=tok: e.matmul(psum[:, :], xT_hi[:, tok], wfc_t[:, :], start=False,
                                                              stop=True), "fc")
            act.after(mm)
            h_read[t % 4] = act.do(lambda e, t=t, psum=psum: e.activation(h_tok[:, t, :], psum[:, :], ACT.Gelu),
                                   "gelu")
            dve.after(h_read[t % 4])
            st = dve.do(lambda e, t=t: e.bn_stats(h_stat[:, t, :], h_tok[:, t, :]), "h_stats")
            dve.after(st)
            h_aggr[t] = dve.do(lambda e, t=t: e.bn_aggr(h_mv[:, t, :], h_stat[:, t, :]), "h_aggr")
        dve.after(h_aggr[-1])
        eps = dve.do(lambda e: e.tensor_scalar(h_rstd, h_mv[:, :, 1], LN_EPS, None, ALU.add), "h_eps")
        act.after(eps)
        root = act.do(lambda e: e.activation(h_rstd, h_rstd, ACT.Sqrt), "h_sqrt")
        dve.after(root)
        h_ready = dve.do(lambda e: e.reciprocal(h_rstd, h_rstd), "h_rstd")
        turn_read, f_mm, stored = [None] * 4, [None] * NC, []
        x3_last = x3_split[-1]

        def ffn_out(c):
            dve.after(h_ready)
            for t in chunk(c):
                normed = dve.do(lambda e, t=t: e.tensor_scalar(h_tok[:, t, :], h_tok[:, t, :], h_mv[:, t, 0:1],
                                                               h_rstd[:, t:t + 1], ALU.subtract, ALU.mult), "h_norm")
            for k in range(NK):
                pe.after(normed, turn_read[k], x3_last)
                for j, t in enumerate(chunk(c)):
                    mm = pe.do(lambda e, j=j, t=t, k=k: e.transpose(
                        bank[k][:, j * P:(j + 1) * P], h_tok[:, t, k * P:(k + 1) * P], ident),
                        "turn_h" if j == CT - 1 else None)
                act.after(mm, f_mm[c - 2] if c >= 2 else None)
                turn_read[k] = act.do(lambda e, k=k: e.activation(
                    hT[c % 2][:, k, :], bank[k][:, :], ACT.Identity, bias=col[:, COL_LNB + k:COL_LNB + k + 1],
                    scale=col[:, COL_LNW + k:COL_LNW + k + 1]), "affine_h")
            psum = bank[4 + c]
            pe.after(turn_read[NK - 1], proj_ready, h_read[c])
            for t in range(CT):
                for k in range(NK):
                    mm = pe.do(lambda e, t=t, k=k: e.matmul(
                        psum[:, t * D:(t + 1) * D], hT[c % 2][:, k, t * P:(t + 1) * P], wpr_t[:, k, :],
                        start=(k == 0), stop=(k == NK - 1)), "ffn_out" if (t, k) == (CT - 1, NK - 1) else None)
            f_mm[c] = mm
            flat = x_tok[:, c * CT:(c + 1) * CT, :].rearrange("p t d -> p (t d)")
            dve.after(mm)
            done = dve.do(lambda e, flat=flat, psum=psum: e.tensor_tensor(flat, flat, psum[:, :], ALU.add), "ffn_res")
            sp.after(done)
            stored.append(sp.do(lambda e, flat=flat, c=c: e.dma_start(out[:, c * CTOK:(c + 1) * CTOK], flat),
                                f"store{c}", 16))

        for c in range(NC):
            ffn_out(c)
        sp.after(*stored)

        block = stack.enter_context(nc.Block())
        block.tensor(pe.play)
        block.scalar(act.play)
        block.vector(dve.play)
        block.gpsimd(pool.play)
        block.sync(sp.play)


def kernel(**inputs):
    import concourse.bacc as bacc
    from concourse.bass_utils import run_bass_kernel_spmd

    a = {k: np.asarray(v) for k, v in inputs.items()}
    n = lambda k: a["L0_" + k]
    lines = lambda m: np.ascontiguousarray(m)
    x = lines(a["x"].reshape(NT, P, D).transpose(1, 0, 2).reshape(P, NT * D))
    ctxT = lines(a["ctx_1024"][:, :T, :].reshape(B * T, D).T)
    chunks = lambda m, k: lines(m.reshape(k, P, -1).transpose(1, 0, 2).reshape(P, -1))
    cols = lines(np.concatenate(
        [n("xattn_bq").reshape(HP, P), n("xattn_bk").reshape(HP, P)]
        + [n("attn_time_maa_" + m).reshape(1, D) for m in "kvrg"]
        + [n("attn_ln_w").reshape(1, D), n("attn_ln_b").reshape(1, D),
           n("ffn_ln_w").reshape(NK, P), n("ffn_ln_b").reshape(NK, P)]).T)
    feeds = {
        "x": x, "ctxT": ctxT, "w_q": n("xattn_Wq"), "w_k": n("xattn_Wk"), "w_v": n("xattn_Wv"),
        "w_o": chunks(n("xattn_Wo"), HP),
        "rows": lines(np.concatenate([n("xattn_bv"), n("xattn_bo")])[None]),
        "dec_u": lines(np.concatenate([n("attn_time_decay").reshape(-1), n("attn_time_faaaa").reshape(-1)])[None]),
        "cols": cols,
        "w_rwkv": lines(np.concatenate([n("attn_W" + m).T for m in "rkvgo"], axis=1)),
        "w_fc": lines(n("ffn_W_fc").T), "w_proj": chunks(n("ffn_W_proj").T, NK),
        "consts": shape_constants(),
    }
    nc = bacc.Bacc("TRN2", target_bir_lowering=False, num_devices=1)
    arrays, args = {}, []
    for name, v in feeds.items():
        v = lines(v)
        arrays[f"in_{name}"] = v
        args.append(nc.dram_tensor(f"in_{name}", v.shape, mybir.dt.from_np(v.dtype), kind="ExternalInput").ap())
    args.append(nc.dram_tensor("out_tok", (P, NT * D), F32, kind="ExternalOutput").ap())
    build_block(nc, *args)
    r = run_bass_kernel_spmd(nc, [arrays], core_ids=[0])
    got = r.results[0]["out_tok"]
    return lines(got.reshape(P, NT, D).transpose(1, 0, 2).reshape(B, T, D))
```

```python
from contextlib import ExitStack

import numpy as np

import concourse.bass as bass
from concourse import mybir

F32 = mybir.dt.float32
F32R = mybir.dt.float32r
ALU = mybir.AluOpType
ACT = mybir.ActivationFunctionType
X = mybir.AxisListType.X

P = 128
B, T, D = 32, 64, 128
NT = B * T // P
H, DK = 16, 64
HP = H // 2
RH, RN = 16, 8
HG = 4
NGR = RH // HG
FH = 512
NK = FH // P
SCALE = DK ** -0.5
GT = 2
NG = NT // GT
GTOK = GT * P
GB = GTOK // T
LN_EPS = 1e-5
GN_EPS = 1e-5 * 64
GAMMA_EPS = 1e-6
RSQRT_SEED = 0x5F3759DF
NEWTON_STEPS = 3
POINTS = 8
STATS_POINT = 6
LN_X, LN_HIDDEN, LN_RWKV, LN_FFN = range(4)
MASKED = -3.0e38
DECAY_CAP = 1e30

COL_BQ, COL_BK, COL_MAA, COL_GNW, COL_GNB, COL_LNW, COL_LNB, NCOL = 0, 8, 16, 20, 21, 22, 26, 30
C_ID, C_CEN, C_AVG, C_ONES, C_CAUSAL, C_EXP, C_LOWER, C_DIAG, C_HEADM, C_GNEPS, NCONST = (
    0, 128, 256, 384, 512, 576, 640, 704, 768, 772, 773)


def shape_constants():
    c = np.zeros((P, NCONST), np.float32)
    i = np.arange(P)
    t = np.arange(T)
    same = (i[:, None] // RN == i[None, :] // RN).astype(np.float32) / RN
    c[:, C_ID:C_CEN] = np.eye(P)
    c[:, C_CEN:C_AVG] = np.eye(P) - same
    c[:, C_AVG:C_ONES] = same
    c[:, C_ONES:C_CAUSAL] = 1.0 / (FH * D)
    c[:, C_CAUSAL:C_EXP] = np.where(t[None, :] > (i % T)[:, None], MASKED, 0.0)
    c[:, C_EXP:C_LOWER] = np.maximum(t[None, :] - (i % T)[:, None] - 1, 0)
    c[:, C_LOWER:C_DIAG] = t[None, :] > (i % T)[:, None]
    c[:, C_DIAG:C_HEADM] = t[None, :] == (i % T)[:, None]
    c[:, C_GNEPS] = GN_EPS
    c[:, C_HEADM:C_GNEPS] = (i[:, None] // RN) % HG == np.arange(HG)[None, :]
    return c


class Ticket:

    def __init__(self, sem, value):
        self.sem, self.value = sem, value


class Queue:

    def __init__(self, name, new_sem):
        self.name, self.new_sem = name, new_sem
        self.steps, self.sems, self.counts, self.seen = [], {}, {}, {}

    def after(self, *tickets):
        for t in tickets:
            if t is not None and self.seen.get(id(t.sem), 0) < t.value:
                self.seen[id(t.sem)] = t.value
                self.steps.append(("wait", t.sem, t.value))

    def do(self, build, stage=None, by=1):
        if stage is None:
            self.steps.append(("run", build, None, 0))
            return None
        if stage not in self.sems:
            self.sems[stage] = self.new_sem(f"{self.name}_{stage}")
            self.counts[stage] = 0
        self.counts[stage] += by
        self.steps.append(("run", build, self.sems[stage], by))
        return Ticket(self.sems[stage], self.counts[stage])

    def play(self, engine):
        for s in self.steps:
            if s[0] == "wait":
                engine.wait_ge(s[1], s[2])
            else:
                made = s[1](engine)
                if s[2] is not None:
                    made.then_inc(s[2], s[3])


def build_block(nc, x, ctxT, w_q, w_k, w_v, w_o, rows, dec_u, cols, w_rwkv, w_fc, w_proj, consts, out):
    with ExitStack() as stack:
        def sb(name, shape, dt=F32):
            return stack.enter_context(nc.sbuf_tensor(name, shape, dt))

        def new_sem(name):
            return stack.enter_context(nc.semaphore(name))

        pe, act, dve, pool, sp = (Queue(n, new_sem) for n in ("pe", "act", "dve", "pool", "sp"))

        const = sb("const", [P, NCONST])
        col = sb("col", [P, NCOL])
        x_tok = sb("x_tok", [P, NT, D])
        cT = sb("cT", [P, B * T])
        w_raw = sb("w_raw", [P, 3, H * DK])
        w_hi = sb("w_hi", [P, 3, H * DK], F32R)
        w_lo = sb("w_lo", [P, 3, H * DK], F32R)
        wo_sb = sb("wo_sb", [P, HP, D])
        bo_bc = sb("bo_bc", [P, D])
        bv_bc = sb("bv_bc", [P, H * DK])
        decu_bc = sb("decu_bc", [P, 2 * RH])
        wrk = sb("wrk", [P, 5, D])
        wmatT = sb("wmatT", [P, RH, T])
        wfc_raw = sb("wfc_raw", [P, FH])
        wpr_raw = sb("wpr_raw", [P, NK * D])
        wfc_t = sb("wfc_t", [P, FH], F32R)
        wpr_t = sb("wpr_t", [P, NK, D])
        gamma = sb("gamma", [P, 6])
        xT_hi, xT_lo, cT_hi, cT_lo = (sb(n, [P, 2, GTOK], F32R) for n in ("xT_hi", "xT_lo", "cT_hi", "cT_lo"))
        x3_hi, x3_lo = (sb(n, [P, GTOK], F32R) for n in ("x3_hi", "x3_lo"))
        q_sb, k_sb = (sb(n, [P, 2, HP, GTOK]) for n in ("q_sb", "k_sb"))
        v_sb = sb("v_sb", [P, 2, GT, H * DK])
        s_sb, e_sb = (sb(n, [P, 2, HP, 2, T]) for n in ("s_sb", "e_sb"))
        pT_sb, o_sb = (sb(n, [P, 2, HP, P]) for n in ("pT_sb", "o_sb"))
        s_max, s_sum, s_rec = (sb(n, [P, 2, HP, 2]) for n in ("s_max", "s_sum", "s_rec"))
        xn_tok = sb("xn_tok", [P, 3, GT, D])
        xs = sb("xs", [P, 2, GB, T + 1])
        xx = sb("xx", [P, GB, T])
        mixed = sb("mixed", [P, 4, GTOK])
        r_exp = w_raw[:, 0, :].rearrange("p (b m i) -> p b m i", m=HG, i=T)
        attw = w_raw[:, 1:3, :].rearrange("p a n -> p (a n)").rearrange("p (g s n) -> p g s n", g=NGR, s=GT)
        kv_sb = sb("kv_sb", [P, 2, 2, GTOK])
        g_sb = sb("g_sb", [P, 2, GTOK])
        yT, yc, sq, sd, zT = (sb(n, [P, GTOK]) for n in ("yT", "yc", "sq", "sd", "zT"))
        h_tok = sb("h_tok", [P, GT, FH])
        hT = sb("hT", [P, NK, GTOK])
        ln_stat = sb("ln_stat", [P, 4, GT, 6])
        ln_mv = sb("ln_mv", [P, 4, GT, 2])
        ln_var = sb("ln_var", [P, 4, GT])
        ln_half = sb("ln_half", [P, 4, GT], mybir.dt.int32)
        ln_y = sb("ln_y", [P, 4, GT])
        ln_a = sb("ln_a", [P, 4, GT])

        bank = [stack.enter_context(nc.psum_tensor(f"bank{i}", [P, 512], F32)) for i in range(8)]
        bank_read = [None] * 8
        bank_turn = [0]

        def take(n=1):
            got = []
            while len(got) < n:
                i = bank_turn[0] % 8
                bank_turn[0] += 1
                if bank_read[i] != "open":
                    pe.after(bank_read[i])
                    bank_read[i] = "open"
                    got.append(i)
            return got

        ident = const[:, C_ID:C_ID + P]
        centre = const[:, C_CEN:C_CEN + P]
        average = const[:, C_AVG:C_AVG + P]
        flat = lambda v: v.rearrange("p t d -> p (t d)")

        def load(queue, name, dst, src):
            return queue.do(lambda e: e.dma_start(dst, src), f"load_{name}", 16)

        xparts = ((0, 1), (1, 2), (2, 4), (4, NG))

        def load_x(i):
            a, b = xparts[i]
            return load(sp, f"x{i}", flat(x_tok[:, a * GT:b * GT, :]), x[:, a * GTOK:b * GTOK])

        def load_c(i):
            a, b = xparts[i]
            return load(sp, f"ctx{i}", cT[:, a * GTOK:b * GTOK], ctxT[:, a * GTOK:b * GTOK])

        part_of = lambda g: next(i for i, (a, b) in enumerate(xparts) if a <= g < b)
        ld_x, ld_c = [load_x(0)], []
        ld_w = [load(act, "wq", w_raw[:, 0, :], w_q)]
        ld_const = load(sp, "const", const[:, :], consts)
        ld_c.append(load_c(0))
        ld_w.append(load(act, "wk", w_raw[:, 1, :], w_k))
        ld_col = load(act, "col", col[:, :], cols)
        ld_w.append(load(act, "wv", w_raw[:, 2, :], w_v))
        ld_x.append(load_x(1))
        ld_c.append(load_c(1))
        ld_bv = load(sp, "bv", bv_bc[:, :], rows[0:1, 0:H * DK].to_broadcast([P, H * DK]))
        ld_bo = load(sp, "bo", bo_bc[:, :], rows[0:1, H * DK:].to_broadcast([P, D]))
        for i in (2, 3):
            ld_x.append(load_x(i))
            ld_c.append(load_c(i))
        ld_wo = load(sp, "wo", wo_sb[:, :, :].rearrange("p c n -> p (c n)"), w_o)
        ld_decu = load(sp, "decu", decu_bc[:, :], dec_u[0:1, :].to_broadcast([P, 2 * RH]))
        ld_wrk = load(sp, "wrk", wrk[:, :, :].rearrange("p a n -> p (a n)"), w_rwkv)
        ld_fc = load(sp, "fc", wfc_raw[:, :], w_fc)
        ld_proj = load(sp, "proj", wpr_raw[:, :], w_proj)

        def ln_stats(n, tiles, ready):
            dve.after(ready)
            for j, tile in enumerate(tiles):
                s = dve.do(lambda e, j=j, tile=tile: e.bn_stats(ln_stat[:, n, j, :], tile), "ln_stats")
            dve.after(s)
            for j in range(GT):
                s = dve.do(lambda e, j=j: e.bn_aggr(ln_mv[:, n, j, :], ln_stat[:, n, j, :]), "ln_aggr")
            dve.after(s)
            s = dve.do(lambda e: e.tensor_scalar(ln_var[:, n, :], ln_mv[:, n, :, 1], LN_EPS, None, ALU.add), "ln_var")
            dve.after(s)
            s = dve.do(lambda e: e.tensor_scalar(ln_half[:, n, :], ln_var[:, n, :].bitcast(mybir.dt.int32), 1, None,
                                                 ALU.logical_shift_right), "ln_half")
            dve.after(s)
            s = dve.do(lambda e: e.tensor_scalar(ln_y[:, n, :].bitcast(mybir.dt.int32), ln_half[:, n, :], -1.0,
                                                 float(RSQRT_SEED), ALU.mult, ALU.add), "ln_seed")
            rsqrt_asked.append((n, s))

        rsqrt_asked, rsqrt_now, rsqrt_ready = [], [], {}

        def newton(last):
            if not rsqrt_now:
                rsqrt_now.extend(rsqrt_asked)
                rsqrt_asked.clear()
            if not rsqrt_now:
                return
            kinds = sorted(n for n, _ in rsqrt_now)
            some = slice(kinds[0], kinds[-1] + 1)
            assert len(kinds) == some.stop - some.start
            y, v, a = ln_y[:, some, :], ln_var[:, some, :], ln_a[:, some, :]
            pool.after(*(s for _, s in rsqrt_now))
            for step in (lambda e: e.tensor_tensor(a, y, y, ALU.mult),
                         lambda e: e.tensor_tensor(a, a, v, ALU.mult),
                         lambda e: e.tensor_scalar(a, a, -0.5, 1.5, ALU.mult, ALU.add),
                         lambda e: e.tensor_tensor(y, y, a, ALU.mult)):
                s = pool.do(step, "newton")
                pool.after(s)
            if last:
                rsqrt_ready.update({n: s for n in kinds})
                rsqrt_now.clear()

        def ln_apply(n, src, dst, stage):
            dve.after(rsqrt_ready.pop(n))
            for j in range(GT):
                s = dve.do(lambda e, j=j: e.tensor_scalar(dst[:, j, :], src[:, j, :], ln_mv[:, n, j, 0:1],
                                                          ln_y[:, n, j:j + 1], ALU.subtract, ALU.mult), stage)
            return s

        def turn_group(psum, src, ready, stage):
            pe.after(ld_const, ready)
            for j in range(GT):
                mm = pe.do(lambda e, j=j: e.transpose(psum[:, j * P:(j + 1) * P], src[:, j, :], ident),
                           stage if j == GT - 1 else None)
            return mm

        def split(raw, hi, lo, ready):
            act.after(*ready)
            rounded = act.do(lambda e: e.activation(hi, raw, ACT.Copy), "split_hi")
            pool.after(rounded, *ready)
            return pool.do(lambda e: e.tensor_tensor(lo, raw, hi.bitcast(F32), ALU.subtract), "split_lo")

        def split_bank(b, hi, lo, turned, free, stage):
            act.after(turned, free)
            rounded = act.do(lambda e: e.activation(hi, bank[b][:, 0:GTOK], ACT.Copy), stage + "_hi")
            dve.after(rounded, free)
            bank_read[b] = dve.do(lambda e: e.tensor_tensor(lo, bank[b][:, 0:GTOK], hi.bitcast(F32), ALU.subtract),
                                  stage + "_lo")
            return bank_read[b]

        w_split = [None] * 3
        xT_split, c_split, x_bo = [None] * NG, [None] * NG, [None] * NG
        q_proj, v_proj = [None] * NG, [None] * NG
        q_done, k_done, v_done = ([None] * NG for _ in range(3))
        qk_used, v_used = [None] * NG, [None] * NG
        s_mm, s_less, exp_done, p_norm, p_turned, pT_done, pv_mm, o_done, wo_mm, res_done = (
            [None] * NT for _ in range(10))
        before = lambda tickets, i, n: tickets[i - n] if i >= n else None

        def wait_rsqrt():
            for _ in range(1 + NEWTON_STEPS):
                yield

        def prefetch(g):
            tiles = x_tok[:, g * GT:(g + 1) * GT, :]
            ln_stats(LN_X, [tiles[:, j, :] for j in range(GT)], ld_x[part_of(g)])
            yield from wait_rsqrt()
            normed = ln_apply(LN_X, tiles, xn_tok[:, 0, :, :], "ln1")
            sl = slice(g * GTOK, (g + 1) * GTOK)
            c_split[g] = split(cT[:, sl], cT_hi[:, g % 2, :], cT_lo[:, g % 2, :],
                               (ld_c[part_of(g)], before(v_proj, g, 2)))
            pool.after(normed, ld_bo)
            x_bo[g] = pool.do(lambda e: e.tensor_tensor(
                tiles, tiles, bo_bc[:, :].unsqueeze(1).to_broadcast([P, GT, D]), ALU.add), "add_bo")
            yield
            b, = take()
            turned = turn_group(bank[b], xn_tok[:, 0, :, :], normed, "turn_x")
            xT_split[g] = split_bank(b, xT_hi[:, g % 2, :], xT_lo[:, g % 2, :], turned, before(q_proj, g, 2),
                                     "split_x")
            yield

        def project_qk(g, which, c):
            b, = take()
            hi, lo = ((xT_hi, xT_lo), (cT_hi, cT_lo))[which]
            pe.after(w_split[which], (xT_split, c_split)[which][g])
            for j in range(2):
                w = slice((2 * c + j) * P, (2 * c + j + 1) * P)
                o = bank[b][:, j * GTOK:(j + 1) * GTOK]
                pe.do(lambda e, w=w, o=o: e.matmul(o, w_hi[:, which, w], lo[:, g % 2, :], start=True, stop=False))
                pe.do(lambda e, w=w, o=o: e.matmul(o, w_lo[:, which, w], hi[:, g % 2, :], start=False, stop=False))
                mm = pe.do(lambda e, w=w, o=o: e.matmul(o, w_hi[:, which, w], hi[:, g % 2, :], start=False,
                                                        stop=True), "project" if j else None)
            if which == 0:
                q_proj[g] = mm
            dst = (q_sb, k_sb)[which]
            bias = (COL_BQ, COL_BK)[which] + 2 * c
            act.after(mm, ld_col, before(qk_used, g, 2))
            for j in range(2):
                done = act.do(lambda e, j=j: e.activation(
                    dst[:, g % 2, 2 * c + j, :], bank[b][:, j * GTOK:(j + 1) * GTOK], ACT.Identity,
                    bias=col[:, bias + j:bias + j + 1]), "project" if j else None)
            bank_read[b] = (q_done, k_done)[which][g] = done

        def project_v(g, n):
            tt, half = n // 2, n % 2
            b, = take()
            tok = slice(tt * P, (tt + 1) * P)
            w = slice(half * 512, half * 512 + 512)
            pe.after(w_split[2], c_split[g])
            o = bank[b][:, :]
            pe.do(lambda e: e.matmul(o, cT_lo[:, g % 2, tok], w_hi[:, 2, w], start=True, stop=False))
            pe.do(lambda e: e.matmul(o, cT_hi[:, g % 2, tok], w_lo[:, 2, w], start=False, stop=False))
            mm = pe.do(lambda e: e.matmul(o, cT_hi[:, g % 2, tok], w_hi[:, 2, w], start=False, stop=True), "project")
            v_proj[g] = mm
            dve.after(mm, ld_bv, before(v_used, g, 2))
            bank_read[b] = v_done[g] = dve.do(lambda e: e.tensor_tensor(
                v_sb[:, g % 2, tt, w], o, bv_bc[:, w], ALU.add), "project")

        def scores(t):
            g, tt, r = t // GT, t % GT, t % 2
            banks = take(2)
            pe.after(q_done[g], k_done[g])
            for c in range(HP):
                for par, b in ((0, 0), (1, 1), (0, 1), (1, 0)):
                    dk = slice(par * DK, par * DK + DK)
                    tok = slice(tt * P + b * T, tt * P + b * T + T)
                    mm = pe.do(lambda e, c=c, b=b, dk=dk, tok=tok: e.matmul(
                        bank[banks[b]][dk, c * T:(c + 1) * T], q_sb[dk, g % 2, c, tok], k_sb[dk, g % 2, c, tok],
                        start=True, stop=True), "scores" if (c, par, b) == (HP - 1, 1, 0) else None)
            s_mm[t] = qk_used[g] = mm
            dve.after(mm, before(exp_done, t, 2))
            causal = const[:, C_CAUSAL:C_CAUSAL + T].unsqueeze(1).to_broadcast([P, HP, T])
            for b in range(2):
                masked = dve.do(lambda e, b=b: e.tensor_tensor(
                    s_sb[:, r, :, b, :], bank[banks[b]][:, :].rearrange("p (c k) -> p c k", c=HP), causal,
                    ALU.add), "mask")
                bank_read[banks[b]] = masked
            dve.after(masked)
            top = dve.do(lambda e: e.tensor_reduce(s_max[:, r, :, :], s_sb[:, r, :, :, :], X, ALU.max), "max")
            pool.after(top)
            s_less[t] = pool.do(lambda e: e.tensor_tensor(
                s_sb[:, r, :, :, :], s_sb[:, r, :, :, :],
                s_max[:, r, :, :].unsqueeze(3).to_broadcast([P, HP, 2, T]), ALU.subtract), "less_max")

        def exponent(t):
            r = t % 2
            act.after(s_less[t], before(p_turned, t, 2))
            exp_done[t] = act.do(lambda e: e.activation(e_sb[:, r, :, :, :], s_sb[:, r, :, :, :], ACT.Exp,
                                                        scale=SCALE), "exp")

        def normalise(t):
            r = t % 2
            dve.after(exp_done[t])
            total = dve.do(lambda e: e.tensor_reduce(s_sum[:, r, :, :], e_sb[:, r, :, :, :], X, ALU.add), "sum")
            dve.after(total)
            rec = dve.do(lambda e: e.reciprocal(s_rec[:, r, :, :], s_sum[:, r, :, :]), "rec")
            pool.after(rec)
            p_norm[t] = pool.do(lambda e: e.tensor_tensor(
                e_sb[:, r, :, :, :], e_sb[:, r, :, :, :],
                s_rec[:, r, :, :].unsqueeze(3).to_broadcast([P, HP, 2, T]), ALU.mult), "normalise")

        def turn_probs(t):
            r = t % 2
            banks = take(2)
            pe.after(p_norm[t])
            act.after(before(pv_mm, t, 2))
            for c in range(HP):
                b = banks[c // 4]
                mm = pe.do(lambda e, b=b, c=c: e.transpose(
                    bank[b][:, (c % 4) * P:(c % 4 + 1) * P], e_sb[:, r, c, :, :].rearrange("p b k -> p (b k)"),
                    ident), "turn_p" if c % 4 == 3 else None)
                if c % 4 == 3:
                    act.after(mm)
                    bank_read[b] = act.do(lambda e, b=b, c=c: e.activation(
                        pT_sb[:, r, c - 3:c + 1, :].rearrange("p c q -> p (c q)"), bank[b][:, :], ACT.Copy),
                        "turn_p")
            p_turned[t], pT_done[t] = mm, bank_read[b]

        def values(t):
            g, tt, r = t // GT, t % GT, t % 2
            banks = take(2)
            pe.after(pT_done[t], v_done[g])
            for c in range(HP):
                for b, par in ((0, 0), (1, 1), (0, 1), (1, 0)):
                    keys = slice(b * T, b * T + T)
                    h = 2 * c + par
                    mm = pe.do(lambda e, c=c, b=b, par=par, keys=keys, h=h: e.matmul(
                        bank[banks[b]][par * DK:par * DK + DK, c * T:(c + 1) * T],
                        v_sb[keys, g % 2, tt, h * DK:(h + 1) * DK], pT_sb[keys, r, c, par * T:par * T + T],
                        start=True, stop=True), "values" if (c, b, par) == (HP - 1, 1, 0) else None)
            pv_mm[t] = v_used[g] = mm
            act.after(mm, before(wo_mm, t, 2))
            for b in range(2):
                bank_read[banks[b]] = o_done[t] = act.do(lambda e, b=b: e.activation(
                    o_sb[:, r, :, b * T:(b + 1) * T], bank[banks[b]][:, :].rearrange("p (c q) -> p c q", c=HP),
                    ACT.Copy), "values")

        def output(t):
            r = t % 2
            b, = take()
            pe.after(o_done[t], ld_wo)
            for c in range(HP):
                mm = pe.do(lambda e, c=c: e.matmul(bank[b][:, 0:D], o_sb[:, r, c, :], wo_sb[:, c, :],
                                                   start=(c == 0), stop=(c == HP - 1)),
                           "output" if c == HP - 1 else None)
            wo_mm[t] = mm
            dve.after(mm, x_bo[t // GT])
            bank_read[b] = res_done[t] = dve.do(lambda e: e.tensor_tensor(
                x_tok[:, t, :], bank[b][:, 0:D], x_tok[:, t, :], ALU.add), "output")

        decay_ready, fc_ready, proj_ready = [None], [None], [None]

        def build_decay():
            heads = lambda c: const[:, c:c + T].unsqueeze(1).to_broadcast([P, RH, T])
            tmp = w_raw[:, 2, :].rearrange("p (h i) -> p h i", h=RH)
            act.after(ld_decu, ld_const)
            a = act.do(lambda e: e.activation(decu_bc[:, 0:RH], decu_bc[:, 0:RH], ACT.Exp), "decay")
            pool.after(a)
            b = pool.do(lambda e: e.tensor_scalar(decu_bc[:, 0:RH], decu_bc[:, 0:RH], DECAY_CAP, -1.0, ALU.min,
                                                  ALU.mult), "decay")
            yield
            act.after(b)
            for h in range(RH):
                a = act.do(lambda e, h=h: e.activation(wmatT[:, h, :], const[:, C_EXP:C_EXP + T], ACT.Exp,
                                                       scale=decu_bc[:, h:h + 1]), "decay")
            yield
            pool.after(a)
            lower = pool.do(lambda e: e.tensor_tensor(wmatT[:, :, :], wmatT[:, :, :], heads(C_LOWER), ALU.mult),
                            "decay_lower")
            yield
            pool.after(w_split[2])
            diag = pool.do(lambda e: e.tensor_tensor(
                tmp, heads(C_DIAG), decu_bc[:, RH:2 * RH].unsqueeze(2).to_broadcast([P, RH, T]), ALU.mult),
                "decay_diag")
            yield
            pool.after(lower, diag)
            decay_ready[0] = pool.do(lambda e: e.tensor_tensor(wmatT[:, :, :], wmatT[:, :, :], tmp, ALU.add),
                                     "decay_sum")
            yield

        def build_ternary(raw, dst, ready, g, result, name):
            scratch = w_raw[:, 2, 0:FH]
            act.after(ready, decay_ready[0], fc_ready[0])
            total = act.do(lambda e: e.activation(scratch, raw, ACT.Abs, accum_out=gamma[:, g:g + 1]), name + "_abs")
            yield
            b, = take()
            pe.after(total, ld_const)
            mean = pe.do(lambda e: e.matmul(bank[b][:, 0:1], const[:, C_ONES:C_ONES + P], gamma[:, g:g + 1],
                                            start=True, stop=True), name + "_mean")
            dve.after(mean)
            up = dve.do(lambda e: e.tensor_scalar(gamma[:, g + 1:g + 2], bank[b][:, 0:1], GAMMA_EPS, 0.5, ALU.add,
                                                  ALU.mult), name + "_thr")
            down = dve.do(lambda e: e.tensor_scalar(gamma[:, g + 2:g + 3], bank[b][:, 0:1], GAMMA_EPS, -0.5,
                                                    ALU.add, ALU.mult), name + "_thr")
            bank_read[b] = down
            dve.after(up, down)
            below = dve.do(lambda e: e.tensor_scalar(scratch, raw, gamma[:, g + 2:g + 3], None, ALU.is_lt),
                           name + "_below")
            dve.after(below)
            result[0] = dve.do(lambda e: e.scalar_tensor_tensor(
                out=dst, in0=raw, scalar=gamma[:, g + 1:g + 2], in1=scratch, op0=ALU.is_gt, op1=ALU.subtract),
                name + "_ternary")
            yield

        def set_up():
            pool.do(lambda e: e.memset(xs[:, :, :, 0:1], 0.0), "zero")
            yield from build_decay()
            yield from build_ternary(wfc_raw[:, :], wfc_t[:, :], ld_fc, 0, fc_ready, "fc")
            yield from build_ternary(wpr_raw[:, :], wpr_t[:, :, :].rearrange("p k n -> p (k n)"), ld_proj, 3,
                                     proj_ready, "proj")

        proj2_mm, att_mm, y_mm, z_mm, fc_mm, turned_h, ffn_mm, xs_mixed = ([None] * NG for _ in range(8))
        stored = []

        def later_stages(g):
            prev = lambda tickets: before(tickets, g, 1)
            tiles = x_tok[:, g * GT:(g + 1) * GT, :]
            ln_stats(LN_RWKV, [tiles[:, j, :] for j in range(GT)], res_done[g * GT + GT - 1])
            yield from wait_rsqrt()
            normed = ln_apply(LN_RWKV, tiles, xn_tok[:, 1, :, :], "ln2")
            yield
            b, = take()
            turned = turn_group(bank[b], xn_tok[:, 1, :, :], normed, "turn_x2")
            now = xs[:, g % 2, :, 1:]
            act.after(turned, before(xs_mixed, g, 2))
            shifted = bank_read[b] = act.do(lambda e: e.activation(
                now, bank[b][:, 0:GTOK].rearrange("p (b t) -> p b t", t=T), ACT.Copy), "xs")
            pool.after(shifted, prev(xs_mixed))
            diff = pool.do(lambda e: e.tensor_tensor(xx[:, :, :], xs[:, g % 2, :, 0:T], now, ALU.subtract), "xx")
            yield
            dve.after(diff, ld_col, prev(proj2_mm))
            for m in range(4):
                mixing = xs_mixed[g] = dve.do(lambda e, m=m: e.scalar_tensor_tensor(
                    out=mixed[:, m, :].rearrange("p (b t) -> p b t", t=T), in0=xx[:, :, :],
                    scalar=col[:, COL_MAA + m:COL_MAA + m + 1], in1=now, op0=ALU.mult, op1=ALU.add), "mix")
            yield
            kv, rg = take(2)
            pe.after(mixing, ld_wrk)
            pe.do(lambda e: e.matmul(bank[kv][:, 0:GTOK], wrk[:, 1, :], mixed[:, 0, :], start=True, stop=True))
            for j in range(GT):
                mm = pe.do(lambda e, j=j: e.matmul(
                    bank[kv][:, GTOK + j * D:GTOK + (j + 1) * D], mixed[:, 1, j * P:(j + 1) * P], wrk[:, 2, :],
                    start=True, stop=True), "rwkv" if j == GT - 1 else None)
            dve.after(mm, before(y_mm, g, 2))
            kv_done = bank_read[kv] = dve.do(lambda e: e.tensor_copy(
                kv_sb[:, g % 2, :, :].rearrange("p a n -> p (a n)"), bank[kv][:, :]), "kv")
            pe.do(lambda e: e.matmul(bank[rg][:, 0:GTOK], wrk[:, 0, :], mixed[:, 2, :], start=True, stop=True))
            mm = pe.do(lambda e: e.matmul(bank[rg][:, GTOK:2 * GTOK], wrk[:, 3, :], mixed[:, 3, :], start=True,
                                          stop=True), "rwkv")
            proj2_mm[g] = mm
            act.after(mm, prev(att_mm), *w_split)
            for m in range(HG):
                r_done = act.do(lambda e, m=m: e.activation(
                    r_exp[:, :, m, :], bank[rg][:, 0:GTOK].rearrange("p (b i) -> p b i", i=T), ACT.Copy,
                    scale=const[:, C_HEADM + m:C_HEADM + m + 1]), "r")
            act.after(before(z_mm, g, 2))
            gate = bank_read[rg] = act.do(lambda e: e.activation(g_sb[:, g % 2, :], bank[rg][:, GTOK:2 * GTOK],
                                                                 ACT.Gelu), "gate")
            kT, v_tok = kv_sb[:, g % 2, 0, :], kv_sb[:, g % 2, 1, :]
            yield
            banks = take(NGR)
            pe.after(r_done, kv_done)
            for tt in range(GT):
                for par in range(2):
                    for n in range(NGR):
                        ch, seq = slice(32 * n, 32 * n + 32), 2 * tt + par
                        mm = pe.do(lambda e, tt=tt, par=par, seq=seq, n=n, ch=ch: e.matmul(
                            bank[banks[n]][par * T:par * T + T, tt * HG * T:(tt + 1) * HG * T],
                            kT[ch, seq * T:(seq + 1) * T], r_exp[ch, seq, :, :], start=True, stop=True,
                            tile_position=(32 * n, par * T)),
                            "attend" if (tt, par, n) == (GT - 1, 1, NGR - 1) else None)
                if tt == 0:
                    yield
            att_mm[g] = mm
            dve.after(mm, decay_ready[0], proj_ready[0], prev(y_mm))
            for n in range(NGR):
                decayed = bank_read[banks[n]] = dve.do(lambda e, n=n: e.tensor_tensor(
                    attw[:, n, :, :], bank[banks[n]][:, :].rearrange("p (s n) -> p s n", s=GT),
                    wmatT[:, HG * n:HG * n + HG, :].rearrange("p h i -> p (h i)").unsqueeze(1)
                    .to_broadcast([P, GT, HG * T]), ALU.mult), "decayed")
            yield
            banks_y = take(2)
            pe.after(decayed)
            for tt in range(GT):
                for n in range(NGR):
                    for par in range(2):
                        mm = pe.do(lambda e, tt=tt, par=par, n=n: e.matmul(
                            bank[banks_y[par]][32 * n:32 * n + 32, tt * HG * T:(tt + 1) * HG * T],
                            v_tok[par * T:par * T + T, tt * D + 32 * n:tt * D + 32 * n + 32],
                            attw[par * T:par * T + T, n, tt, :], start=True, stop=True,
                            tile_position=(par * T, 32 * n)),
                            "mix_values" if (tt, n, par) == (GT - 1, NGR - 1, 1) else None)
                if tt == 0:
                    yield
            y_mm[g] = mm
            y_view = yT[:, :].rearrange("p (t b i) -> p t b i", t=GT, b=2)
            last = [mm, mm]
            for m in range(HG):
                for par in range(2):
                    src = bank[banks_y[par]][:, :].rearrange("p (t m i) -> p t m i", t=GT, m=HG)[:, :, m, :]
                    dst = y_view[:, :, par, :]
                    mask = const[:, C_HEADM + m:C_HEADM + m + 1]
                    dve.after(last[par])
                    if m == 0:
                        last[par] = dve.do(lambda e, src=src, dst=dst, mask=mask: e.tensor_scalar(
                            dst, src, mask, None, ALU.mult), "own_head")
                    else:
                        last[par] = dve.do(lambda e, src=src, dst=dst, mask=mask: e.scalar_tensor_tensor(
                            out=dst, in0=src, scalar=mask, in1=dst, op0=ALU.mult, op1=ALU.add), "own_head")
            bank_read[banks_y[0]], bank_read[banks_y[1]] = last
            yield
            b1, = take()
            pe.after(*last)
            mm = pe.do(lambda e: e.matmul(bank[b1][:, 0:GTOK], centre, yT[:, :], start=True, stop=True), "centre")
            act.after(mm, prev(z_mm))
            squared = act.do(lambda e: e.activation(sq[:, :], bank[b1][:, 0:GTOK], ACT.Square), "square")
            centred = bank_read[b1] = act.do(lambda e: e.activation(yc[:, :], bank[b1][:, 0:GTOK], ACT.Copy),
                                             "centred")
            yield
            b2, = take()
            pe.after(squared)
            mm = pe.do(lambda e: e.matmul(bank[b2][:, 0:GTOK], average, sq[:, :], start=True, stop=True), "variance")
            act.after(mm)
            root = bank_read[b2] = act.do(lambda e: e.activation(
                sd[:, :], bank[b2][:, 0:GTOK], ACT.Sqrt, bias=const[:, C_GNEPS:C_GNEPS + 1]), "gn_sqrt")
            yield
            dve.after(root)
            s = dve.do(lambda e: e.reciprocal(sd[:, :], sd[:, :]), "gn_rec")
            dve.after(s, centred)
            s = dve.do(lambda e: e.tensor_tensor(yc[:, :], yc[:, :], sd[:, :], ALU.mult), "gn")
            dve.after(s)
            s = dve.do(lambda e: e.tensor_scalar(yc[:, :], yc[:, :], col[:, COL_GNW:COL_GNW + 1],
                                                 col[:, COL_GNB:COL_GNB + 1], ALU.mult, ALU.add), "gn_affine")
            dve.after(s, gate)
            gated = dve.do(lambda e: e.tensor_tensor(zT[:, :], yc[:, :], g_sb[:, g % 2, :], ALU.mult), "gated")
            yield
            b3, = take()
            pe.after(gated)
            for j in range(GT):
                mm = pe.do(lambda e, j=j: e.matmul(bank[b3][:, j * D:(j + 1) * D], zT[:, j * P:(j + 1) * P],
                                                   wrk[:, 4, :], start=True, stop=True),
                           "rwkv_out" if j == GT - 1 else None)
            z_mm[g] = mm
            dve.after(mm)
            res2 = bank_read[b3] = dve.do(lambda e: e.tensor_tensor(flat(tiles), flat(tiles), bank[b3][:, 0:GTOK],
                                                                    ALU.add), "rwkv_res")
            yield
            ln_stats(LN_FFN, [tiles[:, j, :] for j in range(GT)], res2)
            yield from wait_rsqrt()
            normed3 = ln_apply(LN_FFN, tiles, xn_tok[:, 2, :, :], "ln3")
            yield
            b4, = take()
            turned3 = turn_group(bank[b4], xn_tok[:, 2, :, :], normed3, "turn_x3")
            x3_split = split_bank(b4, x3_hi[:, :], x3_lo[:, :], turned3, prev(fc_mm), "split_x3")
            yield
            yield
            banks_h = take(GT)
            pe.after(x3_split, fc_ready[0])
            act.after(prev(turned_h))
            for j in range(GT):
                tok = slice(j * P, (j + 1) * P)
                o = bank[banks_h[j]][:, :]
                pe.do(lambda e, o=o, tok=tok: e.matmul(o, x3_lo[:, tok], wfc_t[:, :], start=True, stop=False))
                mm = pe.do(lambda e, o=o, tok=tok: e.matmul(o, x3_hi[:, tok], wfc_t[:, :], start=False, stop=True),
                           "fc")
                act.after(mm)
                gelu = bank_read[banks_h[j]] = act.do(lambda e, j=j, o=o: e.activation(h_tok[:, j, :], o, ACT.Gelu),
                                                      "gelu")
            fc_mm[g] = mm
            yield
            ln_stats(LN_HIDDEN, [h_tok[:, j, :] for j in range(GT)], gelu)
            yield from wait_rsqrt()
            normed4 = ln_apply(LN_HIDDEN, h_tok, h_tok, "ln4")
            yield
            pe.after(normed4)
            for half in range(2):
                b5, = take()
                for kk in range(2):
                    for j in range(GT):
                        k = 2 * half + kk
                        mm = pe.do(lambda e, j=j, k=k, kk=kk, b5=b5: e.transpose(
                            bank[b5][:, kk * GTOK + j * P:kk * GTOK + (j + 1) * P],
                            h_tok[:, j, k * P:(k + 1) * P], ident), "turn_h" if (kk, j) == (1, GT - 1) else None)
                act.after(mm, prev(ffn_mm))
                for kk in range(2):
                    k = 2 * half + kk
                    hT_done = bank_read[b5] = act.do(lambda e, k=k, kk=kk, b5=b5: e.activation(
                        hT[:, k, :], bank[b5][:, kk * GTOK:(kk + 1) * GTOK], ACT.Identity,
                        bias=col[:, COL_LNB + k:COL_LNB + k + 1], scale=col[:, COL_LNW + k:COL_LNW + k + 1]),
                        "affine_h")
            turned_h[g] = mm
            yield
            b6, = take()
            pe.after(hT_done, proj_ready[0])
            for j in range(GT):
                for k in range(NK):
                    mm = pe.do(lambda e, j=j, k=k: e.matmul(
                        bank[b6][:, j * D:(j + 1) * D], hT[:, k, j * P:(j + 1) * P], wpr_t[:, k, :],
                        start=(k == 0), stop=(k == NK - 1)), "ffn_out" if (j, k) == (GT - 1, NK - 1) else None)
            ffn_mm[g] = mm
            dve.after(mm)
            done = bank_read[b6] = dve.do(lambda e: e.tensor_tensor(flat(tiles), flat(tiles), bank[b6][:, 0:GTOK],
                                                                    ALU.add), "ffn_res")
            sp.after(done)
            stored.append(sp.do(lambda e: e.dma_start(out[:, g * GTOK:(g + 1) * GTOK], flat(tiles)),
                                f"store{g}", 16))
            yield

        jobs = []
        for g in range(NG):
            jobs += [lambda g=g, c=c: project_qk(g, 0, c) for c in range(HP // 2)]
            jobs += [lambda g=g, c=c: project_qk(g, 1, c) for c in range(HP // 2)]
            jobs += [lambda g=g, n=n: project_v(g, n) for n in range(2 * GT)]

        def run_jobs(n):
            for _ in range(min(n, len(jobs))):
                jobs.pop(0)()

        chains = []

        points = [0]

        def point(before_steps=(), after_steps=()):
            now = points[0] % POINTS
            since = (now - STATS_POINT) % POINTS
            if 1 <= since <= NEWTON_STEPS:
                newton(since == NEWTON_STEPS)
            for action in before_steps:
                action()
            for chain in list(chains):
                if next(chain, "over") == "over":
                    chains.remove(chain)
            for action in after_steps:
                action()
            points[0] += 1

        def slot(actions, start=()):
            for i in range(POINTS):
                if i == STATS_POINT:
                    chains.extend(start)
                point(*((actions.get(i, ()), ()) if i != POINTS - 1 else ((), actions.get(i, ()))))

        def split_w(i):
            w_split[i] = split(w_raw[:, i, :], w_hi[:, i, :], w_lo[:, i, :], (ld_w[i],))

        go = lambda f, *a: (lambda: f(*a))
        points[0] = STATS_POINT
        chains.append(prefetch(0))
        point()
        point()
        slot({0: [go(split_w, 0)], 4: [go(split_w, 1)], 5: [go(split_w, 2)]}, [prefetch(1)])
        slot({0: [go(run_jobs, 2)], 1: [go(run_jobs, 2)], 2: [go(run_jobs, 2)], 3: [go(run_jobs, 2)],
              4: [go(scores, 0)], 5: [go(run_jobs, 1), go(exponent, 0)], 6: [go(run_jobs, 2), go(normalise, 0)],
              7: [go(run_jobs, 1), go(scores, 1)]}, [prefetch(2), set_up()])
        slot({0: [go(run_jobs, 2)], 1: [go(run_jobs, 2)], 2: [go(run_jobs, 2)]})
        for t in range(NT):
            g = t // GT
            jobs_at = {2: 1, 3: 1, 4: 1, 6: 1, 7: 2} if t % GT == 0 else {0: 2, 1: 2, 3: 1, 4: 1}
            actions = {i: [go(run_jobs, jobs_at.get(i, 0))] for i in range(POINTS)}
            actions[0].insert(0, go(turn_probs, t))
            if t + 1 < NT:
                actions[1].append(go(exponent, t + 1))
                actions[2].append(go(normalise, t + 1))
            actions[2].insert(0, go(values, t))
            actions[5].append(go(output, t))
            if t + 2 < NT:
                actions[7].append(go(scores, t + 2))
            start = []
            if t % GT == 0 and g + 3 < NG:
                start.append(prefetch(g + 3))
            if t % GT == GT - 1:
                start.append(later_stages(g))
            slot(actions, start)
        while chains:
            slot({})
        sp.after(*stored)

        block = stack.enter_context(nc.Block())
        block.tensor(pe.play)
        block.scalar(act.play)
        block.vector(dve.play)
        block.gpsimd(pool.play)
        block.sync(sp.play)


def kernel(**inputs):
    import concourse.bacc as bacc
    from concourse.bass_utils import run_bass_kernel_spmd

    a = {k: np.asarray(v) for k, v in inputs.items()}
    n = lambda k: a["L0_" + k]
    lines = lambda m: np.ascontiguousarray(m)
    x = lines(a["x"].reshape(NT, P, D).transpose(1, 0, 2).reshape(P, NT * D))
    ctxT = lines(a["ctx_1024"][:, :T, :].reshape(B * T, D).T)
    chunks = lambda m, k: lines(m.reshape(k, P, -1).transpose(1, 0, 2).reshape(P, -1))
    cols = lines(np.concatenate(
        [n("xattn_bq").reshape(HP, P), n("xattn_bk").reshape(HP, P)]
        + [n("attn_time_maa_" + m).reshape(1, D) for m in "kvrg"]
        + [n("attn_ln_w").reshape(1, D), n("attn_ln_b").reshape(1, D),
           n("ffn_ln_w").reshape(NK, P), n("ffn_ln_b").reshape(NK, P)]).T)
    feeds = {
        "x": x, "ctxT": ctxT, "w_q": n("xattn_Wq"), "w_k": n("xattn_Wk"), "w_v": n("xattn_Wv"),
        "w_o": chunks(n("xattn_Wo"), HP),
        "rows": lines(np.concatenate([n("xattn_bv"), n("xattn_bo")])[None]),
        "dec_u": lines(np.concatenate([n("attn_time_decay").reshape(-1), n("attn_time_faaaa").reshape(-1)])[None]),
        "cols": cols,
        "w_rwkv": lines(np.concatenate([n("attn_W" + m).T for m in "rkvgo"], axis=1)),
        "w_fc": lines(n("ffn_W_fc").T), "w_proj": chunks(n("ffn_W_proj").T, NK),
        "consts": shape_constants(),
    }
    nc = bacc.Bacc("TRN2", target_bir_lowering=False, num_devices=1)
    arrays, args = {}, []
    for name, v in feeds.items():
        v = lines(v)
        arrays[f"in_{name}"] = v
        args.append(nc.dram_tensor(f"in_{name}", v.shape, mybir.dt.from_np(v.dtype), kind="ExternalInput").ap())
    args.append(nc.dram_tensor("out_tok", (P, NT * D), F32, kind="ExternalOutput").ap())
    build_block(nc, *args)
    r = run_bass_kernel_spmd(nc, [arrays], core_ids=[0])
    got = r.results[0]["out_tok"]
    return lines(got.reshape(P, NT, D).transpose(1, 0, 2).reshape(B, T, D))
```

```python
from contextlib import ExitStack

import numpy as np

import concourse.bass as bass
from concourse import mybir

F32 = mybir.dt.float32
F32R = mybir.dt.float32r
ALU = mybir.AluOpType
ACT = mybir.ActivationFunctionType
X = mybir.AxisListType.X

P = 128
B, T, D = 32, 64, 128
NT = B * T // P
H, DK = 16, 64
HP = H // 2
RH, RN = 16, 8
HG = 4
NGR = RH // HG
FH = 512
NK = FH // P
SCALE = DK ** -0.5
GT = 2
NG = NT // GT
GTOK = GT * P
BATCHES = [(GT * g, GT) for g in range(NG - 1)] + [(NT - 2, 1), (NT - 1, 1)]
GB = GTOK // T
LN_EPS = 1e-5
GN_EPS = 1e-5 * 64
GAMMA_EPS = 1e-6
RSQRT_SEED = 0x5F3759DF + 0x40000000 - 0x400000
NEWTON_STEPS = 3
LN_X, LN_HIDDEN, LN_RWKV, LN_FFN = range(4)
K_FIRST = (1, 0, 2)
PLAN = {'split_w': [-2.94073, -2.8931, -2.83968, -2.73759, -2.71389, -2.58526],
 'build': [-1.80583, -0.57801, -0.50837, -0.39558, -0.16832, 0.23809, 0.3647, 0.40764, 0.45506, 0.52335,
           0.93606, 0.99648, 1.08889, 1.13136, 1.24243, 1.39667, 1.42713],
 'stats_x': [-2.68091],
 'apply_x': [-2.41283],
 'split_c': [-2.11753],
 'add_bo': [-2.07439],
 'turn_x': [-2.19762],
 'project': [-1.58288, -1.58209, -1.57617, -1.56761, -1.50729, -1.50312, -1.45902, -1.45604, -1.34813,
             -1.33729, -1.24921, -1.17576, -0.84309, -0.8206, -0.82041, -0.81512, -0.73285, -0.62811,
             -0.62687, -0.62563, -0.55504, -0.55324, -0.55302, -0.55281],
 'scores': [-0.55287, -0.55147, -0.52701, -0.51326, -0.03392, 0.01116, 0.03771, 0.04282],
 'less_max': [-0.50255, 0.04792],
 'exponent': [-0.40056, 0.21301],
 'normalise': [-0.27943, 0.34416],
 'turn_probs': [0.05696, 0.18123, 0.49815, 0.4982],
 'values': [0.19756, 0.20505, 0.22612, 0.24257, 0.5869, 0.58765, 0.60177, 0.64176],
 'output': [0.35359, 0.37631, 0.72795, 0.78347],
 'stats_2': [0.85291],
 'apply_2': [1.18708],
 'turn_2': [1.2262],
 'shift': [1.2401],
 'mix': [1.25129, 1.27681],
 'rwkv_kv': [1.36063],
 'rwkv_rg': [1.3572],
 'gate': [1.37648],
 'attend': [1.38174, 1.39019, 1.41712, 1.43146],
 'decayed': [1.43161, 1.43555, 1.46642, 1.47336],
 'mix_values': [1.49731, 1.49755, 1.5455, 1.57397],
 'own_head': [1.65548, 1.65819],
 'centring': [1.6852],
 'variance': [1.712],
 'gn_root': [1.7397],
 'gn': [1.77179],
 'rwkv_out': [1.8539],
 'stats_3': [1.89505],
 'apply_3': [2.19586],
 'turn_3': [2.2323],
 'fc': [2.29293, 2.33162],
 'gelu': [2.29639, 2.36131],
 'stats_h': [2.40513],
 'apply_h': [2.66437],
 'turn_h': [2.76094, 2.77844],
 'ffn_out': [2.95022, 3.00519],
 'newton_x': [-2.62386, -2.51284, -2.43878],
 'newton_2': [0.89583, 0.94885, 1.0687],
 'newton_3': [1.94919, 1.97454, 2.193],
 'newton_h': [2.44462, 2.5221, 2.58287],
 'attention starts': [0.0013, 1.0033, 2.0007, 3.0026, 4.006, 5.0066, 6.0035, 7.00303],
 'later starts': [0.0107, 1.0057, 2.0047, 3.0026, 4.005, 5.0026, 6.00725, 6.489, 7.1918],
 'stats_2 of 7': [0.90172],
 'stats_2 of 8': [1.01565],
 'newton_2 of 7': [0.93649, 0.95028, 1.06689],
 'newton_2 of 8': [1.07053, 1.08944, 1.09417],
 'apply_2 of 7': [1.10928],
 'apply_2 of 8': [1.12295],
 'turn_2 of 7': [1.12559],
 'turn_2 of 8': [1.134],
 'shift of 7': [1.17758],
 'shift of 8': [1.14697],
 'mix of 7': [1.21729, 1.22399],
 'mix of 8': [1.16014, 1.1732],
 'rwkv_kv of 7': [1.22712],
 'rwkv_kv of 8': [1.22238],
 'rwkv_rg of 7': [1.28218],
 'rwkv_rg of 8': [1.26863],
 'gate of 7': [1.30771],
 'gate of 8': [1.58109],
 'attend of 7': [1.39534, 1.40288, 1.51546, 2.27619],
 'attend of 8': [1.30561, 1.33574, 1.57633, 2.4282],
 'decayed of 7': [1.47237, 1.47611, 1.48476, 1.50796],
 'decayed of 8': [1.41925, 1.42125, 1.48199, 1.57627],
 'mix_values of 7': [1.48043, 1.51713, 1.52721, 1.84966],
 'mix_values of 8': [1.52232, 1.57614, 1.58098, 2.67339],
 'own_head of 7': [1.62336, 1.66471],
 'own_head of 8': [1.58114, 1.5812],
 'centring of 7': [1.69639],
 'centring of 8': [1.69644],
 'variance of 7': [1.75645],
 'variance of 8': [1.70712],
 'gn_root of 7': [1.80171],
 'gn_root of 8': [1.77514],
 'gn of 7': [1.83315],
 'gn of 8': [1.81624],
 'rwkv_out of 7': [1.88861],
 'rwkv_out of 8': [2.08056],
 'stats_3 of 7': [1.92838],
 'stats_3 of 8': [2.08129],
 'newton_3 of 7': [1.97998, 2.12225, 2.13039],
 'newton_3 of 8': [2.08606, 2.10148, 2.3114],
 'apply_3 of 7': [2.13959],
 'apply_3 of 8': [2.33625],
 'turn_3 of 7': [2.27757],
 'turn_3 of 8': [2.38222],
 'fc of 7': [2.34378, 2.47348],
 'fc of 8': [2.48718, 2.71287],
 'gelu of 7': [2.39087, 2.78312],
 'gelu of 8': [2.52412, 2.84478],
 'stats_h of 7': [2.4392],
 'stats_h of 8': [2.56989],
 'newton_h of 7': [2.4824, 2.50476, 2.53322],
 'newton_h of 8': [2.6339, 2.72168, 2.73669],
 'apply_h of 7': [2.78361],
 'apply_h of 8': [2.76871],
 'turn_h of 7': [2.79126, 2.82088],
 'turn_h of 8': [2.79404, 2.79567],
 'ffn_out of 7': [3.47382, 3.5001],
 'ffn_out of 8': [2.83158, 2.84223],
 'stats_x of 0': [-2.88947],
 'newton_x of 0': [-2.87136, -2.81836, -2.79174],
 'apply_x of 0': [-2.77295],
 'split_c of 0': [-2.94118],
 'add_bo of 0': [-1.8029],
 'turn_x of 0': [-2.69453],
 'project of 0': [-2.90922, -2.86601, -2.83106, -2.78825, -2.72416, -2.69345, -2.56474, -2.41977, -2.4103,
                  -2.39287, -1.88593, -1.79867, -1.78452, -1.77036, -1.48394, -1.48163, -1.15646, -1.10827,
                  -0.81041, -0.71992, -0.53935, -0.52041, -0.49145, -0.47941],
 'scores of 0': [-0.94886, -0.55829, -0.51324, -0.51037, -0.50917, -0.45194, -0.44983, -0.34819],
 'less_max of 0': [-0.51016, 0.23012],
 'exponent of 0': [-0.45233, 0.31729],
 'normalise of 0': [-0.21975, 0.36478],
 'turn_probs of 0': [-0.13527, 0.15045, 0.44887, 0.51845],
 'values of 0': [0.2194, 0.38458, 0.39066, 0.40282, 0.50253, 0.53571, 0.63715, 0.64421],
 'output of 0': [0.44786, 0.60572, 0.85799, 0.86015]}
MASKED = -3.0e38
DECAY_CAP = 1e30

COL_BQ, COL_BK, COL_MAA, COL_GNW, COL_GNB, COL_LNW, COL_LNB, NCOL = 0, 8, 16, 20, 21, 22, 26, 30
C_ID, C_CEN, C_AVG, C_ONES, C_CAUSAL, C_EXP, C_LOWER, C_DIAG, C_HEADM, C_GNEPS, NCONST = (
    0, 128, 256, 384, 512, 576, 640, 704, 768, 772, 773)


def shape_constants():
    c = np.zeros((P, NCONST), np.float32)
    i = np.arange(P)
    t = np.arange(T)
    same = (i[:, None] // RN == i[None, :] // RN).astype(np.float32) / RN
    c[:, C_ID:C_CEN] = np.eye(P)
    c[:, C_CEN:C_AVG] = np.eye(P) - same
    c[:, C_AVG:C_ONES] = same
    c[:, C_ONES:C_CAUSAL] = 1.0 / (FH * D)
    c[:, C_CAUSAL:C_EXP] = np.where(t[None, :] > (i % T)[:, None], MASKED, 0.0)
    c[:, C_EXP:C_LOWER] = np.maximum(t[None, :] - (i % T)[:, None] - 1, 0)
    c[:, C_LOWER:C_DIAG] = t[None, :] > (i % T)[:, None]
    c[:, C_DIAG:C_HEADM] = t[None, :] == (i % T)[:, None]
    c[:, C_GNEPS] = GN_EPS
    c[:, C_HEADM:C_GNEPS] = (i[:, None] // RN) % HG == np.arange(HG)[None, :]
    return c


class Ticket:

    def __init__(self, sem, value):
        self.sem, self.value = sem, value


START = Ticket(None, 0)


class Queue:

    def __init__(self, name, new_sem):
        self.name, self.new_sem = name, new_sem
        self.steps, self.sems, self.counts, self.seen = [], {}, {}, {}

    def after(self, *tickets):
        for t in tickets:
            if t is not START and self.seen.get(id(t.sem), 0) < t.value:
                self.seen[id(t.sem)] = t.value
                self.steps.append(("wait", t.sem, t.value))

    def do(self, build, stage=None, by=1):
        if stage is None:
            self.steps.append(("run", build, None, 0))
            return None
        if stage not in self.sems:
            self.sems[stage] = self.new_sem(f"{self.name}_{stage}")
            self.counts[stage] = 0
        self.counts[stage] += by
        self.steps.append(("run", build, self.sems[stage], by))
        return Ticket(self.sems[stage], self.counts[stage])

    def play(self, engine):
        for s in self.steps:
            if s[0] == "wait":
                engine.wait_ge(s[1], s[2])
            else:
                made = s[1](engine)
                if s[2] is not None:
                    made.then_inc(s[2], s[3])


class Banks:

    def __init__(self, n):
        self.last, self.free = [START] * n, list(range(n))

    def __setitem__(self, i, ticket):
        if i in self.free:
            self.free.remove(i)
        self.last[i] = ticket
        self.free.append(i)

    def __getitem__(self, i):
        return self.last[i]

    def oldest(self):
        return self.free.pop(0)


def build_block(nc, x, ctxT, w_q, w_k, w_v, w_o, rows, dec_u, cols, w_rwkv, w_fc, w_proj, consts, out):
    with ExitStack() as stack:
        def sb(name, shape, dt=F32):
            return stack.enter_context(nc.sbuf_tensor(name, shape, dt))

        def new_sem(name):
            return stack.enter_context(nc.semaphore(name))

        pe, act, dve, pool, sp = (Queue(n, new_sem) for n in ("pe", "act", "dve", "pool", "sp"))

        const = sb("const", [P, NCONST])
        col = sb("col", [P, NCOL])
        x_tok = sb("x_tok", [P, NT, D])
        cT = sb("cT", [P, B * T])
        w_raw = sb("w_raw", [P, 3, H * DK])
        w_hi = sb("w_hi", [P, 3, H * DK], F32R)
        w_lo = sb("w_lo", [P, 3, H * DK], F32R)
        wo_sb = sb("wo_sb", [P, HP, D])
        bo_bc = sb("bo_bc", [P, D])
        bv_bc = sb("bv_bc", [P, H * DK])
        decu_bc = sb("decu_bc", [P, 2 * RH])
        wrk = sb("wrk", [P, 5, D])
        wmatT = sb("wmatT", [P, RH, T])
        wfc_raw = sb("wfc_raw", [P, FH])
        wpr_raw = sb("wpr_raw", [P, NK * D])
        wfc_t = sb("wfc_t", [P, FH], F32R)
        wpr_t = sb("wpr_t", [P, NK, D])
        gamma = sb("gamma", [P, 6])
        xT_hi, xT_lo, cT_hi, cT_lo = (sb(n, [P, 2, GTOK], F32R) for n in ("xT_hi", "xT_lo", "cT_hi", "cT_lo"))
        x3_hi, x3_lo = (sb(n, [P, GTOK], F32R) for n in ("x3_hi", "x3_lo"))
        q_sb, k_sb = (sb(n, [P, 2, HP, GTOK]) for n in ("q_sb", "k_sb"))
        v_sb = sb("v_sb", [P, 2, GT, H * DK])
        s_sb, e_sb = (sb(n, [P, 2, HP, 2, T]) for n in ("s_sb", "e_sb"))
        pT_sb, o_sb = (sb(n, [P, 2, HP, P]) for n in ("pT_sb", "o_sb"))
        s_max, s_sum, s_rec = (sb(n, [P, 2, HP, 2]) for n in ("s_max", "s_sum", "s_rec"))
        xn_tok = sb("xn_tok", [P, 3, GT, D])
        xs = sb("xs", [P, 2, GB, T + 1])
        xx = sb("xx", [P, GB, T])
        mixed = sb("mixed", [P, 4, GTOK])
        r_exp = w_raw[:, 0, :].rearrange("p (b m i) -> p b m i", m=HG, i=T)
        attw = w_raw[:, 1:3, :].rearrange("p a n -> p (a n)").rearrange("p (g s n) -> p g s n", g=NGR, s=GT)
        kv_sb = sb("kv_sb", [P, 2, 2, GTOK])
        g_sb = sb("g_sb", [P, 2, GTOK])
        yT, yc, sq, sd, zT = (sb(n, [P, GTOK]) for n in ("yT", "yc", "sq", "sd", "zT"))
        h_tok = sb("h_tok", [P, GT, FH])
        hT = sb("hT", [P, NK, GTOK])
        ln_stat = sb("ln_stat", [P, 4, GT, 6])
        ln_mv = sb("ln_mv", [P, 4, GT, 2])
        ln_var = sb("ln_var", [P, 4, GT])
        ln_bits = sb("ln_bits", [P, 4, GT], mybir.dt.int32)
        ln_y = sb("ln_y", [P, 4, GT])
        ln_a = sb("ln_a", [P, 4, GT])

        bank = [stack.enter_context(nc.psum_tensor(f"bank{i}", [P, 512], F32)) for i in range(8)]
        bank_read = Banks(8)

        def take(n=1):
            got = [bank_read.oldest() for _ in range(n)]
            pe.after(*(bank_read.last[i] for i in got))
            return got

        ident = const[:, C_ID:C_ID + P]
        centre = const[:, C_CEN:C_CEN + P]
        average = const[:, C_AVG:C_AVG + P]
        flat = lambda v: v.rearrange("p t d -> p (t d)")

        def load(queue, name, dst, src):
            return queue.do(lambda e: e.dma_start(dst, src), f"load_{name}", 16)

        xparts = ((0, 1), (1, 2), (2, 4), (4, NG))

        def load_x(i):
            a, b = xparts[i]
            return load(sp, f"x{i}", flat(x_tok[:, a * GT:b * GT, :]), x[:, a * GTOK:b * GTOK])

        def load_c(i):
            a, b = xparts[i]
            return load(sp, f"ctx{i}", cT[:, a * GTOK:b * GTOK], ctxT[:, a * GTOK:b * GTOK])

        part_of = lambda g: next(i for i, (a, b) in enumerate(xparts) if a <= g < b)
        ld_c, ld_x = [load_c(0)], [load_x(0)]
        ld_w = [START] * 3
        ld_w[1] = load(act, "wk", w_raw[:, 1, :], w_k)
        ld_const = load(sp, "const", const[:, :], consts)
        ld_w[0] = load(act, "wq", w_raw[:, 0, :], w_q)
        ld_col = load(act, "col", col[:, :], cols)
        ld_w[2] = load(act, "wv", w_raw[:, 2, :], w_v)
        ld_x.append(load_x(1))
        ld_c.append(load_c(1))
        ld_bv = load(sp, "bv", bv_bc[:, :], rows[0:1, 0:H * DK].to_broadcast([P, H * DK]))
        ld_bo = load(sp, "bo", bo_bc[:, :], rows[0:1, H * DK:].to_broadcast([P, D]))
        for i in (2, 3):
            ld_x.append(load_x(i))
            ld_c.append(load_c(i))
        ld_wo = load(sp, "wo", wo_sb[:, :, :].rearrange("p c n -> p (c n)"), w_o)
        ld_decu = load(sp, "decu", decu_bc[:, :], dec_u[0:1, :].to_broadcast([P, 2 * RH]))
        ld_wrk = load(sp, "wrk", wrk[:, :, :].rearrange("p a n -> p (a n)"), w_rwkv)
        ld_fc = load(sp, "fc", wfc_raw[:, :], w_fc)
        ld_proj = load(sp, "proj", wpr_raw[:, :], w_proj)

        done = {}

        def of(step, i, *part):
            return START if i < 0 else done[(step, i) + part]

        held = {}

        def ln_stats(n, g, tiles, *ready):
            k = len(tiles)
            dve.after(*ready, of("ln_apply", g - 1, n))
            for j, tile in enumerate(tiles):
                s = dve.do(lambda e, j=j, tile=tile: e.bn_stats(ln_stat[:, n, j, :], tile), "ln_stats")
            dve.after(s)
            for j in range(k):
                s = dve.do(lambda e, j=j: e.bn_aggr(ln_mv[:, n, j, :], ln_stat[:, n, j, :]), "ln_aggr")
            dve.after(s)
            s = dve.do(lambda e: e.tensor_scalar(ln_var[:, n, 0:k], ln_mv[:, n, 0:k, 1], LN_EPS, -0.5, ALU.add, ALU.mult),
                       "ln_var")
            dve.after(s)
            s = dve.do(lambda e: e.tensor_scalar(ln_bits[:, n, 0:k], ln_var[:, n, 0:k].bitcast(mybir.dt.int32), 1, None,
                                                 ALU.logical_shift_right), "ln_bits")
            dve.after(s)
            held["newton tiles", g, n] = k
            held["newton", g, n] = dve.do(lambda e: e.tensor_scalar(
                ln_y[:, n, 0:k].bitcast(mybir.dt.int32), ln_bits[:, n, 0:k], -1.0, float(RSQRT_SEED), ALU.mult,
                ALU.add), "ln_seed")

        def newton(n, g, i):
            k = held["newton tiles", g, n]
            y, v, a = ln_y[:, n, 0:k], ln_var[:, n, 0:k], ln_a[:, n, 0:k]
            s = held["newton", g, n]
            for step in (lambda e: e.tensor_tensor(a, y, v, ALU.mult),
                         lambda e: e.tensor_tensor(a, a, y, ALU.mult),
                         lambda e: e.scalar_tensor_tensor(out=y, in0=a, scalar=1.5, in1=y, op0=ALU.add,
                                                          op1=ALU.mult)):
                dve.after(s)
                s = dve.do(step, "newton")
            held["newton", g, n] = s
            if i == NEWTON_STEPS - 1:
                done["newton", g, n] = s

        def ln_apply(n, g, srcs, dst, free):
            dve.after(of("newton", g, n), free)
            for j, src in enumerate(srcs):
                s = dve.do(lambda e, j=j, src=src: e.tensor_scalar(dst[:, j, :], src, ln_mv[:, n, j, 0:1],
                                                          ln_y[:, n, j:j + 1], ALU.subtract, ALU.mult), "ln_apply")
            done["ln_apply", g, n] = s

        def turn(psum, src, n, ready, stage):
            pe.after(ld_const, ready)
            for j in range(n):
                mm = pe.do(lambda e, j=j: e.transpose(psum[:, j * P:(j + 1) * P], src[:, j, :], ident),
                           stage if j == n - 1 else None)
            return mm

        def split(raw, hi, lo, ready, lo_queue):
            act.after(*ready)
            rounded = act.do(lambda e: e.activation(hi, raw, ACT.Copy), "split_hi")
            lo_queue.after(rounded, *ready)
            return lo_queue.do(lambda e: e.tensor_tensor(lo, raw, hi.bitcast(F32), ALU.subtract), "split_lo")

        def split_bank(b, hi, lo, turned, free, stage):
            act.after(turned, free)
            raw = bank[b][:, 0:hi.shape[-1]]
            rounded = act.do(lambda e: e.activation(hi, raw, ACT.Copy), stage + "_hi")
            dve.after(rounded, free)
            bank_read[b] = dve.do(lambda e: e.tensor_tensor(lo, raw, hi.bitcast(F32), ALU.subtract), stage + "_lo")
            return bank_read[b]

        group_of = lambda g: x_tok[:, g * GT:(g + 1) * GT, :]
        tiles_of = lambda view: [view[:, j, :] for j in range(view.shape[1])]

        def split_w(_, i):
            m, half = K_FIRST[i // 2], slice(i % 2 * 512, i % 2 * 512 + 512)
            done["split_w", m, i % 2] = split(w_raw[:, m, half], w_hi[:, m, half], w_lo[:, m, half], (ld_w[m],), dve)

        def stats_x(g, _):
            ln_stats(LN_X, g, tiles_of(group_of(g)), ld_x[part_of(g)])

        def newton_x(g, i):
            newton(LN_X, g, i)

        def apply_x(g, _):
            ln_apply(LN_X, g, tiles_of(group_of(g)), xn_tok[:, 0, :, :], of("turn_x", g - 1))

        def split_c(g, _):
            sl = slice(g * GTOK, (g + 1) * GTOK)
            done["split_c", g] = split(cT[:, sl], cT_hi[:, g % 2, :], cT_lo[:, g % 2, :],
                                       (ld_c[part_of(g)], of("v_mm", g - 2)), pool)

        def add_bo(g, _):
            pool.after(of("ln_apply", g, LN_X), ld_bo)
            done["add_bo", g] = pool.do(lambda e: e.tensor_tensor(
                group_of(g), group_of(g), bo_bc[:, :].unsqueeze(1).to_broadcast([P, GT, D]), ALU.add), "add_bo")

        def turn_x(g, _):
            b, = take()
            done["turn_x", g] = turn(bank[b], xn_tok[:, 0, :, :], GT, of("ln_apply", g, LN_X), "turn_x")
            done["split_x", g] = split_bank(b, xT_hi[:, g % 2, :], xT_lo[:, g % 2, :], of("turn_x", g),
                                            of("q_mm", g - 2), "split_x")

        def project(g, i):
            which, n, half = K_FIRST[i // HP], i % HP // 2, i % 2
            if which < 2:
                project_qk(g, which, n, half)
            else:
                project_v(g, n, half)

        def project_qk(g, which, n, half):
            if half == 0:
                held["project"], = take()
            b = held["project"]
            hi, lo = ((xT_hi, xT_lo), (cT_hi, cT_lo))[which]
            pe.after(of("split_w", which, n // 2), of(("split_x", "split_c")[which], g))
            w = slice((2 * n + half) * P, (2 * n + half + 1) * P)
            o = bank[b][:, half * GTOK:(half + 1) * GTOK]
            pe.do(lambda e: e.matmul(o, w_hi[:, which, w], lo[:, g % 2, :], start=True, stop=False))
            pe.do(lambda e: e.matmul(o, w_lo[:, which, w], hi[:, g % 2, :], start=False, stop=False))
            mm = pe.do(lambda e: e.matmul(o, w_hi[:, which, w], hi[:, g % 2, :], start=False, stop=True),
                       "project" if half else None)
            if half == 0:
                return
            if (which, n) == (0, HP // 2 - 1):
                done["q_mm", g] = mm
            dst = (q_sb, k_sb)[which]
            bias = (COL_BQ, COL_BK)[which] + 2 * n
            act.after(mm, ld_col, of("scores_mm", 2 * g - 3))
            for j in range(2):
                s = act.do(lambda e, j=j: e.activation(
                    dst[:, g % 2, 2 * n + j, :], bank[b][:, j * GTOK:(j + 1) * GTOK], ACT.Identity,
                    bias=col[:, bias + j:bias + j + 1]), "project" if j else None)
            bank_read[b] = done["qk"[which], g, n] = s

        def project_v(g, n, half):
            tt, which_half = n // 2, n % 2
            tok = slice(tt * P, (tt + 1) * P)
            w = slice(which_half * 512, which_half * 512 + 512)
            if half == 0:
                held["project"], = take()
            b = held["project"]
            o = bank[b][:, :]
            if half == 0:
                pe.after(of("split_w", 2, which_half), of("split_c", g))
                pe.do(lambda e: e.matmul(o, cT_lo[:, g % 2, tok], w_hi[:, 2, w], start=True, stop=False))
                pe.do(lambda e: e.matmul(o, cT_hi[:, g % 2, tok], w_lo[:, 2, w], start=False, stop=False))
                return
            mm = pe.do(lambda e: e.matmul(o, cT_hi[:, g % 2, tok], w_hi[:, 2, w], start=False, stop=True), "project")
            if n == 2 * GT - 1:
                done["v_mm", g] = mm
            dve.after(mm, ld_bv, of("values_mm", 2 * g - 3))
            bank_read[b] = done["v", g, tt, which_half] = dve.do(lambda e: e.tensor_tensor(
                v_sb[:, g % 2, tt, w], o, bv_bc[:, w], ALU.add), "project")

        def scores(g, i):
            tt, n = i // (HP // 2), i % (HP // 2)
            t = g * GT + tt
            r = t % 2
            if n == 0:
                held["scores"] = take(2)
            banks = held["scores"]
            pe.after(of("q", g, n), of("k", g, n))
            for c in (2 * n, 2 * n + 1):
                for par, b in ((0, 0), (1, 1), (0, 1), (1, 0)):
                    dk = slice(par * DK, par * DK + DK)
                    tok = slice(tt * P + b * T, tt * P + b * T + T)
                    mm = pe.do(lambda e, c=c, b=b, dk=dk, tok=tok: e.matmul(
                        bank[banks[b]][dk, c * T:(c + 1) * T], q_sb[dk, g % 2, c, tok], k_sb[dk, g % 2, c, tok],
                        start=True, stop=True), "scores" if (c, par, b) == (HP - 1, 1, 0) else None)
            if n < HP // 2 - 1:
                return
            done["scores_mm", t] = mm
            dve.after(mm, of("exp", t - 2))
            causal = const[:, C_CAUSAL:C_CAUSAL + T].unsqueeze(1).to_broadcast([P, HP, T])
            for b in range(2):
                bank_read[banks[b]] = done["mask", t] = dve.do(lambda e, b=b: e.tensor_tensor(
                    s_sb[:, r, :, b, :], bank[banks[b]][:, :].rearrange("p (c k) -> p c k", c=HP), causal,
                    ALU.add), "mask")

        def less_max(g, i):
            t = g * GT + i
            r = t % 2
            dve.after(of("mask", t))
            top = dve.do(lambda e: e.tensor_reduce(s_max[:, r, :, :], s_sb[:, r, :, :, :], X, ALU.max), "max")
            pool.after(top)
            done["less_max", t] = pool.do(lambda e: e.tensor_tensor(
                s_sb[:, r, :, :, :], s_sb[:, r, :, :, :],
                s_max[:, r, :, :].unsqueeze(3).to_broadcast([P, HP, 2, T]), ALU.subtract), "less_max")

        def exponent(g, i):
            t = g * GT + i
            r = t % 2
            act.after(of("less_max", t), of("turn_p", t - 2))
            done["exp", t] = act.do(lambda e: e.activation(e_sb[:, r, :, :, :], s_sb[:, r, :, :, :], ACT.Exp,
                                                           scale=SCALE), "exp")

        def normalise(g, i):
            t = g * GT + i
            r = t % 2
            dve.after(of("exp", t))
            total = dve.do(lambda e: e.tensor_reduce(s_sum[:, r, :, :], e_sb[:, r, :, :, :], X, ALU.add), "sum")
            dve.after(total)
            rec = dve.do(lambda e: e.reciprocal(s_rec[:, r, :, :], s_sum[:, r, :, :]), "rec")
            pool.after(rec)
            done["normalise", t] = pool.do(lambda e: e.tensor_tensor(
                e_sb[:, r, :, :, :], e_sb[:, r, :, :, :],
                s_rec[:, r, :, :].unsqueeze(3).to_broadcast([P, HP, 2, T]), ALU.mult), "normalise")

        def turn_probs(g, i):
            t, n = g * GT + i // 2, i % 2
            r = t % 2
            b, = take()
            pe.after(of("normalise", t))
            for k in range(4):
                mm = pe.do(lambda e, k=k: e.transpose(
                    bank[b][:, k * P:(k + 1) * P], e_sb[:, r, 4 * n + k, :, :].rearrange("p b k -> p (b k)"),
                    ident), "turn_p" if k == 3 else None)
            if n == 1:
                done["turn_p", t] = mm
            act.after(mm, of("values_mm", t - 2))
            bank_read[b] = done["pT", t, n] = act.do(lambda e: e.activation(
                pT_sb[:, r, 4 * n:4 * n + 4, :].rearrange("p c q -> p (c q)"), bank[b][:, :], ACT.Copy), "turn_p")

        def values(g, i):
            tt, n = i // (HP // 2), i % (HP // 2)
            t = g * GT + tt
            r = t % 2
            if n == 0:
                held["values"] = take(2)
            banks = held["values"]
            pe.after(of("pT", t, n // 2), of("v", g, tt, n // 2))
            for c in (2 * n, 2 * n + 1):
                for b, par in ((0, 0), (1, 1), (0, 1), (1, 0)):
                    keys = slice(b * T, b * T + T)
                    h = 2 * c + par
                    mm = pe.do(lambda e, c=c, b=b, par=par, keys=keys, h=h: e.matmul(
                        bank[banks[b]][par * DK:par * DK + DK, c * T:(c + 1) * T],
                        v_sb[keys, g % 2, tt, h * DK:(h + 1) * DK], pT_sb[keys, r, c, par * T:par * T + T],
                        start=True, stop=True), "values" if (c, b, par) == (HP - 1, 1, 0) else None)
            if n < HP // 2 - 1:
                return
            done["values_mm", t] = mm
            act.after(mm, of("output_mm", t - 2))
            for b in range(2):
                bank_read[banks[b]] = done["values", t] = act.do(lambda e, b=b: e.activation(
                    o_sb[:, r, :, b * T:(b + 1) * T], bank[banks[b]][:, :].rearrange("p (c q) -> p c q", c=HP),
                    ACT.Copy), "values")

        def output(g, i):
            t, n = g * GT + i // 2, i % 2
            r = t % 2
            if n == 0:
                held["output"], = take()
            b = held["output"]
            pe.after(of("values", t), ld_wo)
            for c in range(4 * n, 4 * n + 4):
                mm = pe.do(lambda e, c=c: e.matmul(bank[b][:, 0:D], o_sb[:, r, c, :], wo_sb[:, c, :],
                                                   start=(c == 0), stop=(c == HP - 1)),
                           "output" if c == HP - 1 else None)
            if n == 0:
                return
            done["output_mm", t] = mm
            dve.after(mm, of("add_bo", g))
            bank_read[b] = done["output", t] = dve.do(lambda e: e.tensor_tensor(
                x_tok[:, t, :], bank[b][:, 0:D], x_tok[:, t, :], ALU.add), "output")

        def build_decay():
            tmp = w_raw[:, 2, :].rearrange("p (h i) -> p h i", h=RH)
            act.after(ld_decu, ld_const)
            a = act.do(lambda e: e.activation(decu_bc[:, 0:RH], decu_bc[:, 0:RH], ACT.Exp), "decay")
            pool.after(a)
            b = pool.do(lambda e: e.tensor_scalar(decu_bc[:, 0:RH], decu_bc[:, 0:RH], DECAY_CAP, -1.0, ALU.min,
                                                  ALU.mult), "decay")
            yield
            for h in range(RH):
                act.after(b)
                a = act.do(lambda e, h=h: e.activation(wmatT[:, h, :], const[:, C_EXP:C_EXP + T], ACT.Exp,
                                                       scale=decu_bc[:, h:h + 1]), "decay")
                if h % 4 == 3:
                    yield
            for part in (slice(0, RH // 2), slice(RH // 2, RH)):
                wm, tm = wmatT[:, part, :], tmp[:, part, :]
                heads = lambda c: const[:, c:c + T].unsqueeze(1).to_broadcast([P, RH // 2, T])
                pool.after(a)
                lower = pool.do(lambda e, wm=wm: e.tensor_tensor(wm, wm, heads(C_LOWER), ALU.mult), "decay_lower")
                yield
                pool.after(of("split_w", 2, 0), of("split_w", 2, 1))
                diag = pool.do(lambda e, tm=tm, part=part: e.tensor_tensor(
                    tm, heads(C_DIAG), decu_bc[:, RH:2 * RH][:, part].unsqueeze(2).to_broadcast([P, RH // 2, T]),
                    ALU.mult), "decay_diag")
                yield
                pool.after(lower, diag)
                done["decay", 0] = pool.do(lambda e, wm=wm, tm=tm: e.tensor_tensor(wm, wm, tm, ALU.add),
                                           "decay_sum")
                yield

        def build_ternary(raw, dst, ready, free, g, name):
            scratch = w_raw[:, 2, 0:FH]
            act.after(ready, free)
            total = act.do(lambda e: e.activation(scratch, raw, ACT.Abs, accum_out=gamma[:, g:g + 1]), name + "_abs")
            yield
            b, = take()
            pe.after(total, ld_const)
            mean = pe.do(lambda e: e.matmul(bank[b][:, 0:1], const[:, C_ONES:C_ONES + P], gamma[:, g:g + 1],
                                            start=True, stop=True), name + "_mean")
            dve.after(mean)
            up = dve.do(lambda e: e.tensor_scalar(gamma[:, g + 1:g + 2], bank[b][:, 0:1], GAMMA_EPS, 0.5, ALU.add,
                                                  ALU.mult), name + "_thr")
            down = dve.do(lambda e: e.tensor_scalar(gamma[:, g + 2:g + 3], bank[b][:, 0:1], GAMMA_EPS, -0.5,
                                                    ALU.add, ALU.mult), name + "_thr")
            bank_read[b] = down
            yield
            dve.after(up, down)
            below = dve.do(lambda e: e.tensor_scalar(scratch, raw, gamma[:, g + 2:g + 3], None, ALU.is_lt),
                           name + "_below")
            dve.after(below)
            done[name, 0] = dve.do(lambda e: e.scalar_tensor_tensor(
                out=dst, in0=raw, scalar=gamma[:, g + 1:g + 2], in1=scratch, op0=ALU.is_gt, op1=ALU.subtract),
                name + "_ternary")
            yield

        def build_all():
            done["zero", 0] = pool.do(lambda e: e.memset(xs[:, :, :, 0:1], 0.0), "zero")
            yield from build_decay()
            yield from build_ternary(wfc_raw[:, :], wfc_t[:, :], ld_fc, of("decay", 0), 0, "fc_ready")
            yield from build_ternary(wpr_raw[:, :], wpr_t[:, :, :].rearrange("p k n -> p (k n)"), ld_proj,
                                     of("fc_ready", 0), 3, "proj_ready")

        building = build_all()

        first_tile, n_tiles = (list(v) for v in zip(*BATCHES))
        n_tok = lambda g: n_tiles[g] * P
        rows_of = lambda g: x_tok[:, first_tile[g]:first_tile[g] + n_tiles[g], :]

        def stats_2(g, _):
            ln_stats(LN_RWKV, g, tiles_of(rows_of(g)), *(of("output", first_tile[g] + j) for j in range(n_tiles[g])))

        def newton_2(g, i):
            newton(LN_RWKV, g, i)

        def apply_2(g, _):
            ln_apply(LN_RWKV, g, tiles_of(rows_of(g)), xn_tok[:, 1, :, :], of("turn_2", g - 1))

        xs_now = lambda g: xs[:, g % 2, 0:2 * n_tiles[g], 1:]

        def turn_2(g, _):
            b, = take()
            done["turn_2", g] = turn(bank[b], xn_tok[:, 1, :, :], n_tiles[g], of("ln_apply", g, LN_RWKV), "turn_x2")
            act.after(of("turn_2", g), of("mix", g - 2, 1))
            bank_read[b] = done["xs", g] = act.do(lambda e: e.activation(
                xs_now(g), bank[b][:, 0:n_tok(g)].rearrange("p (b t) -> p b t", t=T), ACT.Copy), "xs")

        def shift(g, _):
            pool.after(of("zero", 0), of("xs", g), of("mix", g - 1, 1))
            done["xx", g] = pool.do(lambda e: e.tensor_tensor(xx[:, 0:2 * n_tiles[g], :], xs[:, g % 2, 0:2 * n_tiles[g], 0:T], xs_now(g),
                                                              ALU.subtract), "xx")

        def mix(g, i):
            dve.after(of("xx", g), ld_col, of("rwkv_mm", g - 1))
            for m in (2 * i, 2 * i + 1):
                done["mix", g, i] = dve.do(lambda e, m=m: e.scalar_tensor_tensor(
                    out=mixed[:, m, 0:n_tok(g)].rearrange("p (b t) -> p b t", t=T), in0=xx[:, 0:2 * n_tiles[g], :],
                    scalar=col[:, COL_MAA + m:COL_MAA + m + 1], in1=xs_now(g), op0=ALU.mult, op1=ALU.add), "mix")

        def rwkv_kv(g, _):
            b, = take()
            pe.after(of("mix", g, 0), ld_wrk)
            w, n = n_tok(g), n_tiles[g]
            pe.do(lambda e: e.matmul(bank[b][:, 0:w], wrk[:, 1, :], mixed[:, 0, 0:w], start=True, stop=True))
            for j in range(n):
                mm = pe.do(lambda e, j=j: e.matmul(
                    bank[b][:, w + j * D:w + (j + 1) * D], mixed[:, 1, j * P:(j + 1) * P], wrk[:, 2, :],
                    start=True, stop=True), "rwkv" if j == n - 1 else None)
            dve.after(mm, of("mix_values_mm", g - 2))
            done["kv", g] = bank_read[b] = dve.do(lambda e: e.tensor_copy(
                kv_sb[:, g % 2, :, 0:w], bank[b][:, 0:2 * w].rearrange("p (a n) -> p a n", a=2)), "kv")

        def rwkv_rg(g, _):
            b, = take()
            held["rg", g] = b
            pe.after(of("mix", g, 1), of("mix", g, 0), ld_wrk)
            w = n_tok(g)
            pe.do(lambda e: e.matmul(bank[b][:, 0:w], wrk[:, 0, :], mixed[:, 2, 0:w], start=True, stop=True))
            mm = pe.do(lambda e: e.matmul(bank[b][:, w:2 * w], wrk[:, 3, :], mixed[:, 3, 0:w], start=True,
                                          stop=True), "rwkv")
            done["rg_mm", g] = mm
            act.after(mm, of("attend_mm", g - 1), *(of("split_w", m, i) for m in range(3) for i in range(2)))
            for m in range(HG):
                done["r", g] = act.do(lambda e, m=m: e.activation(
                    r_exp[:, 0:2 * n_tiles[g], m, :], bank[b][:, 0:w].rearrange("p (b i) -> p b i", i=T), ACT.Copy,
                    scale=const[:, C_HEADM + m:C_HEADM + m + 1]), "r")
            done["rwkv_mm", g] = mm

        def gate(g, _):
            b = held["rg", g]
            act.after(of("rg_mm", g), of("gated", g - 2))
            done["gate", g] = bank_read[b] = act.do(lambda e: e.activation(
                g_sb[:, g % 2, 0:n_tok(g)], bank[b][:, n_tok(g):2 * n_tok(g)], ACT.Gelu), "gate")

        def attend(g, i):
            tt, par = i // 2, i % 2
            seq, last = i, 2 * n_tiles[g] - 1
            if i > last:
                return
            kT = kv_sb[:, g % 2, 0, :]
            if i == 0:
                held["attend"] = take(NGR)
            banks = held["attend"]
            pe.after(of("r", g), of("kv", g))
            for n in range(NGR):
                ch = slice(32 * n, 32 * n + 32)
                mm = pe.do(lambda e, n=n, ch=ch: e.matmul(
                    bank[banks[n]][par * T:par * T + T, tt * HG * T:(tt + 1) * HG * T],
                    kT[ch, seq * T:(seq + 1) * T], r_exp[ch, seq, :, :], start=True, stop=True,
                    tile_position=(32 * n, par * T)), "attend" if (i, n) == (last, NGR - 1) else None)
            if i == last:
                done["attend_mm", g] = mm

        def decayed(g, n):
            b, k = held["attend"][n], n_tiles[g]
            dve.after(of("attend_mm", g), of("decay", 0), of("proj_ready", 0), of("mix_values_mm", g - 1))
            bank_read[b] = done["decayed", g] = dve.do(lambda e: e.tensor_tensor(
                attw[:, n, 0:k, :], bank[b][:, 0:k * HG * T].rearrange("p (s n) -> p s n", s=k),
                wmatT[:, HG * n:HG * n + HG, :].rearrange("p h i -> p (h i)").unsqueeze(1)
                .to_broadcast([P, k, HG * T]), ALU.mult), "decayed")
            done["decayed", g, n] = done["decayed", g]

        def mix_values(g, i):
            tt = i % 2
            last = n_tiles[g] + 1
            if tt >= n_tiles[g]:
                return
            v_tok = kv_sb[:, g % 2, 1, :]
            if i == 0:
                held["mix_values"] = take(2)
            banks = held["mix_values"]
            for n in (2 * (i // 2), 2 * (i // 2) + 1):
                pe.after(of("decayed", g, n))
                for par in range(2):
                    mm = pe.do(lambda e, par=par, n=n: e.matmul(
                        bank[banks[par]][32 * n:32 * n + 32, tt * HG * T:(tt + 1) * HG * T],
                        v_tok[par * T:par * T + T, tt * D + 32 * n:tt * D + 32 * n + 32],
                        attw[par * T:par * T + T, n, tt, :], start=True, stop=True,
                        tile_position=(par * T, 32 * n)),
                        "mix_values" if (i, n, par) == (last, NGR - 1, 1) else None)
            if i == last:
                done["mix_values_mm", g] = mm

        def own_head(g, par):
            k = n_tiles[g]
            y_view = yT[:, 0:n_tok(g)].rearrange("p (t b i) -> p t b i", t=k, b=2)
            b = held["mix_values"][par]
            s = of("mix_values_mm", g)
            dve.after(of("centre", g - 1))
            for m in range(HG):
                src = bank[b][:, 0:k * HG * T].rearrange("p (t m i) -> p t m i", t=k, m=HG)[:, :, m, :]
                dst = y_view[:, :, par, :]
                mask = const[:, C_HEADM + m:C_HEADM + m + 1]
                dve.after(s)
                if m == 0:
                    s = dve.do(lambda e, src=src, dst=dst, mask=mask: e.tensor_scalar(
                        dst, src, mask, None, ALU.mult), "own_head")
                else:
                    s = dve.do(lambda e, src=src, dst=dst, mask=mask: e.scalar_tensor_tensor(
                        out=dst, in0=src, scalar=mask, in1=dst, op0=ALU.mult, op1=ALU.add), "own_head")
            bank_read[b] = done["own_head", g, par] = s

        def centring(g, _):
            b, = take()
            pe.after(of("own_head", g, 0), of("own_head", g, 1))
            mm = pe.do(lambda e: e.matmul(bank[b][:, 0:n_tok(g)], centre, yT[:, 0:n_tok(g)], start=True, stop=True), "centre")
            done["centre", g] = mm
            act.after(mm, of("variance_mm", g - 1), of("gated", g - 1))
            done["square", g] = act.do(lambda e: e.activation(sq[:, 0:n_tok(g)], bank[b][:, 0:n_tok(g)], ACT.Square), "square")
            done["centred", g] = bank_read[b] = act.do(lambda e: e.activation(yc[:, 0:n_tok(g)], bank[b][:, 0:n_tok(g)],
                                                                              ACT.Copy), "centred")

        def variance(g, _):
            b, = take()
            held["variance"] = b
            pe.after(of("square", g))
            done["variance_mm", g] = pe.do(lambda e: e.matmul(bank[b][:, 0:n_tok(g)], average, sq[:, 0:n_tok(g)], start=True,
                                                              stop=True), "variance")

        def gn_root(g, _):
            b = held["variance"]
            act.after(of("variance_mm", g), of("gated", g - 1))
            done["gn_root", g] = bank_read[b] = act.do(lambda e: e.activation(
                sd[:, 0:n_tok(g)], bank[b][:, 0:n_tok(g)], ACT.Sqrt, bias=const[:, C_GNEPS:C_GNEPS + 1]), "gn_sqrt")

        def gn(g, _):
            dve.after(of("gn_root", g))
            s = dve.do(lambda e: e.reciprocal(sd[:, 0:n_tok(g)], sd[:, 0:n_tok(g)]), "gn_rec")
            dve.after(s, of("centred", g))
            s = dve.do(lambda e: e.scalar_tensor_tensor(out=yc[:, 0:n_tok(g)], in0=yc[:, 0:n_tok(g)], scalar=col[:, COL_GNW:COL_GNW + 1],
                                                        in1=sd[:, 0:n_tok(g)], op0=ALU.mult, op1=ALU.mult), "gn")
            dve.after(s, of("gate", g), of("rwkv_out_mm", g - 1))
            done["gated", g] = dve.do(lambda e: e.scalar_tensor_tensor(
                out=zT[:, 0:n_tok(g)], in0=yc[:, 0:n_tok(g)], scalar=col[:, COL_GNB:COL_GNB + 1], in1=g_sb[:, g % 2, 0:n_tok(g)], op0=ALU.add,
                op1=ALU.mult), "gated")

        def rwkv_out(g, _):
            b, = take()
            pe.after(of("gated", g))
            for j in range(n_tiles[g]):
                mm = pe.do(lambda e, j=j: e.matmul(bank[b][:, j * D:(j + 1) * D], zT[:, j * P:(j + 1) * P],
                                                   wrk[:, 4, :], start=True, stop=True),
                           "rwkv_out" if j == n_tiles[g] - 1 else None)
            done["rwkv_out_mm", g] = mm
            dve.after(mm)
            done["rwkv_out", g] = bank_read[b] = dve.do(lambda e: e.tensor_tensor(
                flat(rows_of(g)), flat(rows_of(g)), bank[b][:, 0:n_tok(g)], ALU.add), "rwkv_res")

        def stats_3(g, _):
            ln_stats(LN_FFN, g, tiles_of(rows_of(g)), of("rwkv_out", g))

        def newton_3(g, i):
            newton(LN_FFN, g, i)

        def apply_3(g, _):
            ln_apply(LN_FFN, g, tiles_of(rows_of(g)), xn_tok[:, 2, :, :], of("turn_3", g - 1))

        def turn_3(g, _):
            b, = take()
            done["turn_3", g] = turn(bank[b], xn_tok[:, 2, :, :], n_tiles[g], of("ln_apply", g, LN_FFN), "turn_x3")
            done["split_3", g] = split_bank(b, x3_hi[:, 0:n_tok(g)], x3_lo[:, 0:n_tok(g)], of("turn_3", g), of("fc_mm", g - 1),
                                            "split_x3")

        def fc(g, j):
            if j >= n_tiles[g]:
                return
            b, = take()
            held["fc", g, j] = b
            pe.after(of("split_3", g), of("fc_ready", 0))
            tok = slice(j * P, (j + 1) * P)
            pe.do(lambda e: e.matmul(bank[b][:, :], x3_lo[:, tok], wfc_t[:, :], start=True, stop=False))
            done["fc_mm", g, j] = pe.do(lambda e: e.matmul(
                bank[b][:, :], x3_hi[:, tok], wfc_t[:, :], start=False, stop=True), "fc")
            if j == n_tiles[g] - 1:
                done["fc_mm", g] = done["fc_mm", g, j]

        def gelu(g, j):
            if j >= n_tiles[g]:
                return
            b = held["fc", g, j]
            act.after(of("fc_mm", g, j), of("turn_h", g - 1, 1))
            bank_read[b] = done["gelu", g, j] = act.do(lambda e: e.activation(h_tok[:, j, :], bank[b][:, :],
                                                                              ACT.Gelu), "gelu")

        def stats_h(g, _):
            ln_stats(LN_HIDDEN, g, tiles_of(h_tok[:, 0:n_tiles[g], :]), *(of("gelu", g, j) for j in range(n_tiles[g])))

        def newton_h(g, i):
            newton(LN_HIDDEN, g, i)

        def apply_h(g, _):
            ln_apply(LN_HIDDEN, g, tiles_of(h_tok[:, 0:n_tiles[g], :]), h_tok, START)

        def turn_h(g, half):
            b, = take()
            pe.after(of("ln_apply", g, LN_HIDDEN))
            for kk in range(2):
                for j in range(n_tiles[g]):
                    k = 2 * half + kk
                    mm = pe.do(lambda e, j=j, k=k, kk=kk: e.transpose(
                        bank[b][:, kk * GTOK + j * P:kk * GTOK + (j + 1) * P],
                        h_tok[:, j, k * P:(k + 1) * P], ident),
                        "turn_h" if (kk, j) == (1, n_tiles[g] - 1) else None)
            done["turn_h", g, half] = mm
            act.after(mm, of("ffn_out_mm", g - 1))
            for kk in range(2):
                k = 2 * half + kk
                done["hT", g, half] = bank_read[b] = act.do(lambda e, k=k, kk=kk: e.activation(
                    hT[:, k, 0:n_tok(g)], bank[b][:, kk * GTOK:kk * GTOK + n_tok(g)], ACT.Identity,
                    bias=col[:, COL_LNB + k:COL_LNB + k + 1], scale=col[:, COL_LNW + k:COL_LNW + k + 1]), "affine_h")

        def ffn_out(g, j):
            last = n_tiles[g] - 1
            if j > last:
                return
            if j == 0:
                held["ffn_out"], = take()
            b = held["ffn_out"]
            pe.after(of("hT", g, 0), of("proj_ready", 0))
            for k in range(NK):
                if k == 2:
                    pe.after(of("hT", g, 1))
                mm = pe.do(lambda e, k=k: e.matmul(
                    bank[b][:, j * D:(j + 1) * D], hT[:, k, j * P:(j + 1) * P], wpr_t[:, k, :],
                    start=(k == 0), stop=(k == NK - 1)), "ffn_out" if (j, k) == (last, NK - 1) else None)
            if j < last:
                return
            done["ffn_out_mm", g] = mm
            dve.after(mm)
            bank_read[b] = result = dve.do(lambda e: e.tensor_tensor(
                flat(rows_of(g)), flat(rows_of(g)), bank[b][:, 0:n_tok(g)], ALU.add), "ffn_res")
            sp.after(result)
            stored.append(sp.do(lambda e: e.dma_start(out[:, first_tile[g] * P:first_tile[g] * P + n_tok(g)], flat(rows_of(g))),
                                f"store{g}", 16))

        stored = []

        set_up = {"split_w": split_w, "build": lambda g, i: next(building)}
        attention = (stats_x, newton_x, apply_x, split_c, add_bo, turn_x, project, scores, less_max, exponent,
                     normalise, turn_probs, values, output)
        later = (stats_2, newton_2, apply_2, turn_2, shift, mix, rwkv_kv, rwkv_rg, gate, attend, decayed,
                 mix_values, own_head, centring, variance, gn_root, gn, rwkv_out, stats_3, newton_3, apply_3,
                 turn_3, fc, gelu, stats_h, newton_h, apply_h, turn_h, ffn_out)
        queue = [(at, 0, i, action) for name, action in set_up.items() for i, at in enumerate(PLAN[name])]
        for steps, starts in ((attention, PLAN["attention starts"]), (later, PLAN["later starts"])):
            for action in steps:
                for g, start in enumerate(starts):
                    name = action.__name__
                    times = PLAN.get(f"{name} of {g}", PLAN[name])
                    queue += [(start + at, g, i, action) for i, at in enumerate(times)]
        for _, g, i, action in sorted(queue, key=lambda entry: entry[0]):
            action(g, i)
        sp.after(*stored)

        block = stack.enter_context(nc.Block())
        block.tensor(pe.play)
        block.scalar(act.play)
        block.vector(dve.play)
        block.gpsimd(pool.play)
        block.sync(sp.play)


def kernel(**inputs):
    import concourse.bacc as bacc
    from concourse.bass_utils import run_bass_kernel_spmd

    a = {k: np.asarray(v) for k, v in inputs.items()}
    n = lambda k: a["L0_" + k]
    lines = lambda m: np.ascontiguousarray(m)
    x = lines(a["x"].reshape(NT, P, D).transpose(1, 0, 2).reshape(P, NT * D))
    ctxT = lines(a["ctx_1024"][:, :T, :].reshape(B * T, D).T)
    chunks = lambda m, k: lines(m.reshape(k, P, -1).transpose(1, 0, 2).reshape(P, -1))
    cols = lines(np.concatenate(
        [n("xattn_bq").reshape(HP, P), n("xattn_bk").reshape(HP, P)]
        + [n("attn_time_maa_" + m).reshape(1, D) for m in "kvrg"]
        + [n("attn_ln_w").reshape(1, D), n("attn_ln_b").reshape(1, D),
           n("ffn_ln_w").reshape(NK, P), n("ffn_ln_b").reshape(NK, P)]).T)
    feeds = {
        "x": x, "ctxT": ctxT, "w_q": n("xattn_Wq"), "w_k": n("xattn_Wk"), "w_v": n("xattn_Wv"),
        "w_o": chunks(n("xattn_Wo"), HP),
        "rows": lines(np.concatenate([n("xattn_bv"), n("xattn_bo")])[None]),
        "dec_u": lines(np.concatenate([n("attn_time_decay").reshape(-1), n("attn_time_faaaa").reshape(-1)])[None]),
        "cols": cols,
        "w_rwkv": lines(np.concatenate([n("attn_W" + m).T for m in "rkvgo"], axis=1)),
        "w_fc": lines(n("ffn_W_fc").T), "w_proj": chunks(n("ffn_W_proj").T, NK),
        "consts": shape_constants(),
    }
    nc = bacc.Bacc("TRN2", target_bir_lowering=False, num_devices=1)
    arrays, args = {}, []
    for name, v in feeds.items():
        v = lines(v)
        arrays[f"in_{name}"] = v
        args.append(nc.dram_tensor(f"in_{name}", v.shape, mybir.dt.from_np(v.dtype), kind="ExternalInput").ap())
    args.append(nc.dram_tensor("out_tok", (P, NT * D), F32, kind="ExternalOutput").ap())
    build_block(nc, *args)
    r = run_bass_kernel_spmd(nc, [arrays], core_ids=[0])
    got = r.results[0]["out_tok"]
    return lines(got.reshape(P, NT, D).transpose(1, 0, 2).reshape(B, T, D))
```
